# Optimizing a Trainium2 kernel written in Bass

```python
import numpy as np
import jax
import jax.numpy as jnp

def _softmax(x, axis=-1):
    return jax.nn.softmax(x, axis=axis)

def _gelu(x):
    return jax.nn.gelu(x, approximate=True)

def _silu(x):
    return jax.nn.silu(x)

def _sigmoid(x):
    return jax.nn.sigmoid(x)

def _layernorm(x, axis=-1, eps=1e-05):
    m = jnp.mean(x, axis=axis, keepdims=True)
    v = jnp.var(x, axis=axis, keepdims=True)
    return (x - m) / jnp.sqrt(v + eps)

def _scatter_add(tgt, idx, src, axis=0):
    return tgt.at[idx].add(src)

def _segment_sum(src, seg, n):
    return jax.ops.segment_sum(src, seg, n)
kernel_name = 'mk_adaln_d1_jaxref_r8_8c77eb'

def setup_inputs(seed: int=0):
    np.random.seed(seed)
    _w = jnp.asarray

    def _L0_attn_setup():
        import jax, jax.numpy as jnp
        import numpy as np
        NUM_HEAD = 16
        D_Q = 64
        D_KV = 64
        ROPE_BASE = 10000.0

        def _cos_sin(seq_len, dim):
            pos = jnp.arange(seq_len, dtype=jnp.float32)[:, None]
            ids = jnp.arange(dim // 2, dtype=jnp.float32)
            theta = ROPE_BASE ** (-2.0 * ids) / (dim // 2)
            r = pos * theta[None, :]
            return (jnp.cos(r), jnp.sin(r))

        def _rope(x, cos, sin):
            b, s, d = x.shape
            xv = x.reshape(b, s, d // 2, 2)
            x0, x1 = (xv[..., 0], xv[..., 1])
            out = jnp.stack([x0 * cos - x1 * sin, x1 * cos + x0 * sin], axis=-1)
            return out.reshape(b, s, d)
        key = jax.random.key(seed)
        ks = jax.random.split(key, 10)
        d_model, d_q, d_kv = (128, D_Q, D_KV)
        b, s = (2, 256)
        w = lambda k, i, o: jax.random.normal(k, (i, o), dtype=jnp.float32) * 0.02
        return {'x': jax.random.normal(ks[0], (b, s, d_model), dtype=jnp.float32), 'Wd_q_w': w(ks[1], d_model, d_q), 'Wd_q_b': jnp.zeros((d_q,), jnp.float32), 'Wu_q_w': w(ks[2], d_q, d_model), 'Wu_q_b': jnp.zeros((d_model,), jnp.float32), 'Wq_r_w': w(ks[3], d_q, d_model), 'Wq_r_b': jnp.zeros((d_model,), jnp.float32), 'Wk_r_w': w(ks[4], d_model, d_model), 'Wk_r_b': jnp.zeros((d_model,), jnp.float32), 'Wd_kv_w': w(ks[5], d_model, d_kv), 'Wd_kv_b': jnp.zeros((d_kv,), jnp.float32), 'Wu_k_w': w(ks[6], d_kv, d_model), 'Wu_k_b': jnp.zeros((d_model,), jnp.float32), 'Wu_v_w': w(ks[7], d_kv, d_model), 'Wu_v_b': jnp.zeros((d_model,), jnp.float32), 'Wo_w': w(ks[8], d_model, d_model), 'Wo_b': jnp.zeros((d_model,), jnp.float32)}
    _L0_attn_in = _L0_attn_setup()

    def _L0_ffn_setup():
        import jax, jax.numpy as jnp
        import numpy as np
        DIM = 128
        DEPTH = 6
        HEADS = 16
        DIM_HEAD = 64
        WINDOW = 32
        INNER = HEADS * DIM_HEAD
        DIM_INNER = int(DIM * 4 * 2 / 3)
        QK_SCALE = 8.0

        def shift_tokens(t):
            a, s = jnp.split(t, 2, -1)
            s = jnp.pad(s, ((0, 0), (1, 0), (0, 0)))[:, :-1]
            return jnp.concatenate([a, s], -1)

        def l2norm(t):
            return t / jnp.maximum(jnp.linalg.norm(t, axis=-1, keepdims=True), 1e-12)

        def rotate_half(x):
            x1, x2 = jnp.split(x, 2, -1)
            return jnp.concatenate([-x2, x1], -1)

        def rotary_tables(n):
            half = jnp.arange(0, DIM_HEAD, 2, dtype=jnp.float32)
            inv_freq = 1.0 / 10000.0 ** (half / DIM_HEAD)
            t = jnp.arange(n, dtype=jnp.float32)
            freqs = t[:, None] * inv_freq[None, :]
            freqs = jnp.concatenate([freqs, freqs], -1)
            base_scale = (half + 0.4 * DIM_HEAD) / (1.4 * DIM_HEAD)
            power = (t - n // 2) / (WINDOW // 2)
            scale = base_scale[None, :] ** power[:, None]
            scale = jnp.concatenate([scale, scale], -1)
            return (freqs, scale)

        def local_attention(q, k, v):
            b, h, n, d = q.shape
            w = WINDOW
            nw = n // w
            bq = q.reshape(b, h, nw, w, d)
            bk = k.reshape(b, h, nw, w, d)
            bv = v.reshape(b, h, nw, w, d)

            def look(t):
                p = jnp.pad(t, ((0, 0), (0, 0), (1, 0), (0, 0), (0, 0)))
                return jnp.concatenate([p[:, :, :nw], p[:, :, 1:]], axis=3)
            bk2, bv2 = (look(bk), look(bv))
            seq = jnp.arange(n).reshape(nw, w)
            seq_p = jnp.pad(seq, ((1, 0), (0, 0)), constant_values=-1)
            jt = jnp.concatenate([seq_p[:nw], seq_p[1:]], axis=1)
            it = seq[:, :, None]
            jb = jt[:, None, :]
            mask = (it < jb) | (it > jb + w) | (jb == -1)
            sim = jnp.einsum('bhwie,bhwje->bhwij', bq, bk2) * QK_SCALE
            sim = jnp.where(mask, -jnp.finfo(sim.dtype).max, sim)
            attn = jax.nn.softmax(sim, -1)
            out = jnp.einsum('bhwij,bhwje->bhwie', attn, bv2)
            return out.reshape(b, h, n, d)

        def attn_layer(x, Wqkv, qs, ksc, Wo):
            b, n, _ = x.shape
            qkv = x @ Wqkv
            q, k, v = jnp.split(qkv, 3, -1)
            sh = lambda t: t.reshape(b, n, HEADS, DIM_HEAD).transpose(0, 2, 1, 3)
            q, k, v = (sh(q), sh(k), sh(v))
            q = l2norm(q) * qs
            k = l2norm(k) * ksc
            freqs, scale = rotary_tables(n)
            cos, sin = (jnp.cos(freqs), jnp.sin(freqs))
            q = q * cos * scale + rotate_half(q) * sin * scale
            inv = 1.0 / scale
            k = k * cos * inv + rotate_half(k) * sin * inv
            out = local_attention(q, k, v)
            out = out.transpose(0, 2, 1, 3).reshape(b, n, INNER)
            return out @ Wo

        def ffn_layer(x, g, bln, W1, b1, W2, b2):
            mu = x.mean(-1, keepdims=True)
            var = ((x - mu) ** 2).mean(-1, keepdims=True)
            xn = (x - mu) / jnp.sqrt(var + 1e-05) * g + bln
            hg = xn @ W1 + b1
            a, gate = jnp.split(hg, 2, -1)
            return a * jax.nn.gelu(gate, approximate=False) @ W2 + b2
        key = jax.random.key(seed)
        ks = jax.random.split(key, 8)
        B, N = (2, 256)
        init = lambda k, shape: jax.random.normal(k, shape, jnp.float32) * 0.02
        return {'x': jax.random.normal(ks[0], (B, N, DIM), jnp.float32), 'Wqkv': init(ks[1], (DEPTH, DIM, 3 * INNER)), 'q_scale': jnp.ones((DEPTH, DIM_HEAD), jnp.float32), 'k_scale': jnp.ones((DEPTH, DIM_HEAD), jnp.float32), 'Wo': init(ks[2], (DEPTH, INNER, DIM)), 'ln_g': jnp.ones((DEPTH, DIM), jnp.float32), 'ln_b': jnp.zeros((DEPTH, DIM), jnp.float32), 'W1': init(ks[3], (DEPTH, DIM, 2 * DIM_INNER)), 'b1': jnp.zeros((DEPTH, 2 * DIM_INNER), jnp.float32), 'W2': init(ks[4], (DEPTH, DIM_INNER, DIM)), 'b2': jnp.zeros((DEPTH, DIM), jnp.float32)}
    _L0_ffn_in = _L0_ffn_setup()
    _L0_c = _w((lambda *s: np.random.randn(*s).astype(np.float32) * 0.05)(4, 128))
    _L0_wmod = _w((lambda *s: np.random.randn(*s).astype(np.float32) * 0.05)(128, 6 * 128) * 128 ** (-0.5))
    _d = {'L0_attn_x': _L0_attn_in['x'], 'L0_attn_Wd_q_w': _L0_attn_in['Wd_q_w'], 'L0_attn_Wd_q_b': _L0_attn_in['Wd_q_b'], 'L0_attn_Wu_q_w': _L0_attn_in['Wu_q_w'], 'L0_attn_Wu_q_b': _L0_attn_in['Wu_q_b'], 'L0_attn_Wq_r_w': _L0_attn_in['Wq_r_w'], 'L0_attn_Wq_r_b': _L0_attn_in['Wq_r_b'], 'L0_attn_Wk_r_w': _L0_attn_in['Wk_r_w'], 'L0_attn_Wk_r_b': _L0_attn_in['Wk_r_b'], 'L0_attn_Wd_kv_w': _L0_attn_in['Wd_kv_w'], 'L0_attn_Wd_kv_b': _L0_attn_in['Wd_kv_b'], 'L0_attn_Wu_k_w': _L0_attn_in['Wu_k_w'], 'L0_attn_Wu_k_b': _L0_attn_in['Wu_k_b'], 'L0_attn_Wu_v_w': _L0_attn_in['Wu_v_w'], 'L0_attn_Wu_v_b': _L0_attn_in['Wu_v_b'], 'L0_attn_Wo_w': _L0_attn_in['Wo_w'], 'L0_attn_Wo_b': _L0_attn_in['Wo_b'], 'L0_ffn_Wqkv': _L0_ffn_in['Wqkv'], 'L0_ffn_q_scale': _L0_ffn_in['q_scale'], 'L0_ffn_k_scale': _L0_ffn_in['k_scale'], 'L0_ffn_Wo': _L0_ffn_in['Wo'], 'L0_ffn_ln_g': _L0_ffn_in['ln_g'], 'L0_ffn_ln_b': _L0_ffn_in['ln_b'], 'L0_ffn_W1': _L0_ffn_in['W1'], 'L0_ffn_b1': _L0_ffn_in['b1'], 'L0_ffn_W2': _L0_ffn_in['W2'], 'L0_ffn_b2': _L0_ffn_in['b2'], 'L0_c': _L0_c, 'L0_wmod': _L0_wmod}
    _x0 = _d['L0_attn_x']
    _d['L0_attn_x'] = jax.random.normal(jax.random.fold_in(jax.random.key(seed), 1), (4, 512, 128), dtype=_x0.dtype)
    del _x0
    return _d

def reference(L0_attn_x, L0_attn_Wd_q_w, L0_attn_Wd_q_b, L0_attn_Wu_q_w, L0_attn_Wu_q_b, L0_attn_Wq_r_w, L0_attn_Wq_r_b, L0_attn_Wk_r_w, L0_attn_Wk_r_b, L0_attn_Wd_kv_w, L0_attn_Wd_kv_b, L0_attn_Wu_k_w, L0_attn_Wu_k_b, L0_attn_Wu_v_w, L0_attn_Wu_v_b, L0_attn_Wo_w, L0_attn_Wo_b, L0_ffn_Wqkv, L0_ffn_q_scale, L0_ffn_k_scale, L0_ffn_Wo, L0_ffn_ln_g, L0_ffn_ln_b, L0_ffn_W1, L0_ffn_b1, L0_ffn_W2, L0_ffn_b2, L0_c, L0_wmod):

    def _L0_attn_ref(x, Wd_q_w, Wd_q_b, Wu_q_w, Wu_q_b, Wq_r_w, Wq_r_b, Wk_r_w, Wk_r_b, Wd_kv_w, Wd_kv_b, Wu_k_w, Wu_k_b, Wu_v_w, Wu_v_b, Wo_w, Wo_b):
        import jax, jax.numpy as jnp
        import numpy as np
        NUM_HEAD = 16
        D_Q = 64
        D_KV = 64
        ROPE_BASE = 10000.0

        def _cos_sin(seq_len, dim):
            pos = jnp.arange(seq_len, dtype=jnp.float32)[:, None]
            ids = jnp.arange(dim // 2, dtype=jnp.float32)
            theta = ROPE_BASE ** (-2.0 * ids) / (dim // 2)
            r = pos * theta[None, :]
            return (jnp.cos(r), jnp.sin(r))

        def _rope(x, cos, sin):
            b, s, d = x.shape
            xv = x.reshape(b, s, d // 2, 2)
            x0, x1 = (xv[..., 0], xv[..., 1])
            out = jnp.stack([x0 * cos - x1 * sin, x1 * cos + x0 * sin], axis=-1)
            return out.reshape(b, s, d)
        b, s, d_model = x.shape
        h = NUM_HEAD
        hd = d_model // h
        scale = jnp.sqrt(jnp.float32(h + D_KV + D_Q))

        def heads(t):
            return t.reshape(b, s, h, hd).transpose(0, 2, 1, 3)
        cos, sin = _cos_sin(s, d_model)
        ct_q = x @ Wd_q_w + Wd_q_b
        qt_c = heads(ct_q @ Wu_q_w + Wu_q_b)
        qt_r = heads(_rope(ct_q @ Wq_r_w + Wq_r_b, cos, sin))
        query = qt_c + qt_r
        ct_kv = x @ Wd_kv_w + Wd_kv_b
        kt_c = heads(ct_kv @ Wu_k_w + Wu_k_b)
        kt_r = heads(_rope(x @ Wk_r_w + Wk_r_b, cos, sin))
        key = kt_c + kt_r
        value = heads(ct_kv @ Wu_v_w + Wu_v_b)
        attn = jnp.einsum('bhqd,bhkd->bhqk', query, key) / scale
        attn = jax.nn.softmax(attn, axis=-1)
        out = jnp.einsum('bhqk,bhkd->bhqd', attn, value)
        out = out.transpose(0, 2, 1, 3).reshape(b, s, d_model)
        return out @ Wo_w + Wo_b

    def _L0_ffn_ref(x, Wqkv, q_scale, k_scale, Wo, ln_g, ln_b, W1, b1, W2, b2):
        import jax, jax.numpy as jnp
        import numpy as np
        DIM = 128
        DEPTH = 6
        HEADS = 16
        DIM_HEAD = 64
        WINDOW = 32
        INNER = HEADS * DIM_HEAD
        DIM_INNER = int(DIM * 4 * 2 / 3)
        QK_SCALE = 8.0

        def shift_tokens(t):
            a, s = jnp.split(t, 2, -1)
            s = jnp.pad(s, ((0, 0), (1, 0), (0, 0)))[:, :-1]
            return jnp.concatenate([a, s], -1)

        def l2norm(t):
            return t / jnp.maximum(jnp.linalg.norm(t, axis=-1, keepdims=True), 1e-12)

        def rotate_half(x):
            x1, x2 = jnp.split(x, 2, -1)
            return jnp.concatenate([-x2, x1], -1)

        def rotary_tables(n):
            half = jnp.arange(0, DIM_HEAD, 2, dtype=jnp.float32)
            inv_freq = 1.0 / 10000.0 ** (half / DIM_HEAD)
            t = jnp.arange(n, dtype=jnp.float32)
            freqs = t[:, None] * inv_freq[None, :]
            freqs = jnp.concatenate([freqs, freqs], -1)
            base_scale = (half + 0.4 * DIM_HEAD) / (1.4 * DIM_HEAD)
            power = (t - n // 2) / (WINDOW // 2)
            scale = base_scale[None, :] ** power[:, None]
            scale = jnp.concatenate([scale, scale], -1)
            return (freqs, scale)

        def local_attention(q, k, v):
            b, h, n, d = q.shape
            w = WINDOW
            nw = n // w
            bq = q.reshape(b, h, nw, w, d)
            bk = k.reshape(b, h, nw, w, d)
            bv = v.reshape(b, h, nw, w, d)

            def look(t):
                p = jnp.pad(t, ((0, 0), (0, 0), (1, 0), (0, 0), (0, 0)))
                return jnp.concatenate([p[:, :, :nw], p[:, :, 1:]], axis=3)
            bk2, bv2 = (look(bk), look(bv))
            seq = jnp.arange(n).reshape(nw, w)
            seq_p = jnp.pad(seq, ((1, 0), (0, 0)), constant_values=-1)
            jt = jnp.concatenate([seq_p[:nw], seq_p[1:]], axis=1)
            it = seq[:, :, None]
            jb = jt[:, None, :]
            mask = (it < jb) | (it > jb + w) | (jb == -1)
            sim = jnp.einsum('bhwie,bhwje->bhwij', bq, bk2) * QK_SCALE
            sim = jnp.where(mask, -jnp.finfo(sim.dtype).max, sim)
            attn = jax.nn.softmax(sim, -1)
            out = jnp.einsum('bhwij,bhwje->bhwie', attn, bv2)
            return out.reshape(b, h, n, d)

        def attn_layer(x, Wqkv, qs, ksc, Wo):
            b, n, _ = x.shape
            qkv = x @ Wqkv
            q, k, v = jnp.split(qkv, 3, -1)
            sh = lambda t: t.reshape(b, n, HEADS, DIM_HEAD).transpose(0, 2, 1, 3)
            q, k, v = (sh(q), sh(k), sh(v))
            q = l2norm(q) * qs
            k = l2norm(k) * ksc
            freqs, scale = rotary_tables(n)
            cos, sin = (jnp.cos(freqs), jnp.sin(freqs))
            q = q * cos * scale + rotate_half(q) * sin * scale
            inv = 1.0 / scale
            k = k * cos * inv + rotate_half(k) * sin * inv
            out = local_attention(q, k, v)
            out = out.transpose(0, 2, 1, 3).reshape(b, n, INNER)
            return out @ Wo

        def ffn_layer(x, g, bln, W1, b1, W2, b2):
            mu = x.mean(-1, keepdims=True)
            var = ((x - mu) ** 2).mean(-1, keepdims=True)
            xn = (x - mu) / jnp.sqrt(var + 1e-05) * g + bln
            hg = xn @ W1 + b1
            a, gate = jnp.split(hg, 2, -1)
            return a * jax.nn.gelu(gate, approximate=False) @ W2 + b2
        for i in range(DEPTH):
            x = attn_layer(shift_tokens(x), Wqkv[i], q_scale[i], k_scale[i], Wo[i]) + x
            x = ffn_layer(shift_tokens(x), ln_g[i], ln_b[i], W1[i], b1[i], W2[i], b2[i]) + x
        return x
    x = L0_attn_x
    mod = (_silu(L0_c) @ L0_wmod).reshape(L0_c.shape[0], 6, 1, -1)
    sa, ca, ga, sb, cb, gb = (mod[:, 0], mod[:, 1], mod[:, 2], mod[:, 3], mod[:, 4], mod[:, 5])
    ga = (2 * (ga >= 0) - 1) * jnp.maximum(jnp.abs(ga), 0.25)
    gb = (2 * (gb >= 0) - 1) * jnp.maximum(jnp.abs(gb), 0.25)
    h = _layernorm(x, axis=-1) * (1 + ca) + sa
    x = x + ga * _L0_attn_ref(h, L0_attn_Wd_q_w, L0_attn_Wd_q_b, L0_attn_Wu_q_w, L0_attn_Wu_q_b, L0_attn_Wq_r_w, L0_attn_Wq_r_b, L0_attn_Wk_r_w, L0_attn_Wk_r_b, L0_attn_Wd_kv_w, L0_attn_Wd_kv_b, L0_attn_Wu_k_w, L0_attn_Wu_k_b, L0_attn_Wu_v_w, L0_attn_Wu_v_b, L0_attn_Wo_w, L0_attn_Wo_b)
    h = _layernorm(x, axis=-1) * (1 + cb) + sb
    x = x + gb * _L0_ffn_ref(h, L0_ffn_Wqkv, L0_ffn_q_scale, L0_ffn_k_scale, L0_ffn_Wo, L0_ffn_ln_g, L0_ffn_ln_b, L0_ffn_W1, L0_ffn_b1, L0_ffn_W2, L0_ffn_b2)
    return x

_drawn_inputs = setup_inputs


def setup_inputs(seed=0):
    import zlib

    import numpy as np

    out = dict(_drawn_inputs(seed))
    spreads = {'L0_attn_Wd_q_b': (0.0, 0.8),
     'L0_attn_Wu_q_b': (0.0, 0.8),
     'L0_attn_Wq_r_b': (0.0, 0.8),
     'L0_attn_Wk_r_b': (0.0, 2.0),
     'L0_attn_Wd_kv_b': (0.0, 0.8),
     'L0_attn_Wu_k_b': (0.0, 2.0),
     'L0_attn_Wu_v_b': (0.0, 0.8),
     'L0_attn_Wo_b': (0.0, 0.316),
     'L0_ffn_q_scale': (1.0, 0.6),
     'L0_ffn_k_scale': (1.0, 0.6),
     'L0_ffn_ln_g': (1.0, 0.6),
     'L0_ffn_ln_b': (0.0, 0.8),
     'L0_ffn_b1': (0.0, 0.8),
     'L0_ffn_b2': (0.0, 0.683)}
    factors = {'L0_attn_Wd_q_w': 8.0,
     'L0_attn_Wu_q_w': 8.0,
     'L0_attn_Wq_r_w': 8.0,
     'L0_attn_Wk_r_w': 8.0,
     'L0_attn_Wd_kv_w': 8.0,
     'L0_attn_Wu_k_w': 8.0,
     'L0_attn_Wu_v_w': 8.0,
     'L0_attn_Wo_w': 8.0,
     'L0_ffn_W1': 7.374,
     'L0_ffn_W2': 7.234}
    for name, (base, spread) in spreads.items():
        noise = np.random.default_rng([zlib.crc32(name.encode()), seed]).standard_normal(out[name].shape)
        drawn = base * np.exp(spread * noise) if base else spread * noise
        out[name] = jnp.asarray(drawn.astype(out[name].dtype))
    for name, factor in factors.items():
        out[name] = (out[name] * factor).astype(out[name].dtype)
    return out
```

```python
from contextlib import ExitStack

import numpy as np
import concourse.bass as bass
from concourse import mybir

F32 = mybir.dt.float32
F32R = mybir.dt.float32r
BF16 = mybir.dt.bfloat16
ALU = mybir.AluOpType
ACT = mybir.ActivationFunctionType
AX_X = mybir.AxisListType.X

P = 128
B, T, D = 4, 512, 128
TT = T // P
AH, AD = 16, 8
AQ = 64
AG = 4
NG = AH // AG
DEPTH, H, DH, WIN = 6, 16, 64, 32
INNER = H * DH
HP = H // 2
NWIN = T // WIN
DI = int(D * 4 * 2 / 3)
DI_CHUNKS = [(c, min(P, DI - c)) for c in range(0, DI, P)]
NC = len(DI_CHUNKS)
EPS = 1e-5
NEG = -1e30

WQ, WK, WV, WQS, WKS = 0, INNER, 2 * INNER, 3 * INNER, 4 * INNER
WCOLS = 5 * INNER

VEC = {}
for _n in ("bq_c", "bq_r", "bq_s", "bk_c", "bk_r", "bk_s", "b_o", "b_dq", "b_dkv"):
    VEC[_n] = len(VEC)
for _i in range(DEPTH):
    for _n in ("qs", "qs_s", "ks", "ks_s", "g", "b", "b2"):
        VEC[_n, _i] = len(VEC)
    for _c in range(NC):
        VEC["b1a", _i, _c] = len(VEC)
        VEC["b1g", _i, _c] = len(VEC)
NVEC = len(VEC)


class Engine:

    def __init__(self):
        self.steps, self.sem, self.count, self.waited = [], None, 0, {}

    def start_stage(self, sem):
        self.sem, self.count = sem, 0

    def wait(self, *marks):
        for m in marks:
            if isinstance(m, (list, tuple)) and m and isinstance(m[0], (list, tuple, type(None))):
                self.wait(*m)
            elif m:
                sem, value = m
                if self.waited.get(sem.name, 0) < value:
                    self.waited[sem.name] = value
                    self.steps.append(lambda e, s=sem, v=value: e.wait_ge(s, v))

    def do(self, fn, *after, signal=True):
        self.wait(*after)
        if not signal:
            self.steps.append(fn)
            return None
        self.count += 1
        sem = self.sem
        self.steps.append(lambda e: fn(e).then_inc(sem, 1))
        return (sem, self.count)

    def dma(self, fn, sem, *after):
        self.wait(*after)
        self.steps.append(lambda e: fn(e).then_inc(sem, 16))

    def last(self):
        return (self.sem, self.count) if self.count else None


class Banks:

    def __init__(self, banks):
        self.banks, self.free, self.at = banks, [None] * len(banks), 0

    def take(self):
        i = self.at % len(self.banks)
        self.at += 1
        return i, self.banks[i], self.free[i]


def build(nc, a, out):
    ctx = ExitStack()
    sem = lambda name: ctx.enter_context(nc.semaphore(name))

    def sb(scope, name, shape, dt=F32):
        return scope.enter_context(nc.sbuf_tensor(name, shape, dt))

    pe, dve, act, pool, sp = (Engine() for _ in range(5))
    engines = {"pe": pe, "dve": dve, "act": act, "pool": pool}

    def start_stage(n):
        ends = [e.last() for e in engines.values()]
        for name, e in engines.items():
            e.start_stage(sem(f"s_{name}_{n}"))
        for e in engines.values():
            e.wait(ends)
        return ends

    psum = ctx.enter_context(nc.psum_tensor("psum", [P, 8, 512], F32))
    bank = lambda i: psum[:, i, :]

    ident = sb(ctx, "ident", [P, P])
    vecs = sb(ctx, "vecs", [P, NVEC])
    xT = sb(ctx, "xT", [P, B, T])
    rT = sb(ctx, "rT", [P, B, T])
    mod = sb(ctx, "mod", [P, 6, B])
    stats = sb(ctx, "stats", [P, TT, 6])
    mv = sb(ctx, "mv", [P, TT, 2])
    rstd = sb(ctx, "rstd", [P, TT])
    epsc = sb(ctx, "epsc", [P, 1])
    xn = sb(ctx, "xn", [P, TT, P])

    s_const, s_a, s_out = sem("s_const"), sem("s_a"), sem("s_out")
    s_wraw = [sem("s_wqkv0"), sem("s_wqkv1")]
    s_wffn = [sem(f"s_wffn{i}") for i in range(DEPTH)]
    vec = lambda key, n=P: vecs[0:n, VEC[key]:VEC[key] + 1]

    sp.dma(lambda e: e.dma_start(ident[:, :], a["ident"]), s_const)
    sp.dma(lambda e: e.dma_start(vecs[:, :], a["vecs"]), s_const)
    consts = (s_const, 32)

    def transpose_tiles(bank_out, src, n_part=P, after=()):
        for t in range(TT):
            m = pe.do(lambda e, t=t: e.transpose(bank_out[:, t * P:(t + 1) * P], src(t), ident[:, :]),
                      after, consts, signal=t == TT - 1)
        return m

    xn_free = [None]

    def normalise(src, ready):
        for t in range(TT):
            m = dve.do(lambda e, t=t: e.bn_stats(stats[:, t, :], src(t)), ready, dve.last())
        for t in range(TT):
            m2 = dve.do(lambda e, t=t: e.bn_aggr(mv[:, t, :], stats[:, t, :]), m)
        m = act.do(lambda e: e.activation(rstd[:, :], mv[:, :, 1], ACT.Sqrt, bias=epsc[:, 0:1]), m2, eps_set)
        m = dve.do(lambda e: e.reciprocal(rstd[:, :], rstd[:, :]), m)
        for t in range(TT):
            r = dve.do(lambda e, t=t: e.tensor_scalar(xn[:, t, :], src(t), mv[:, t, 0:1], rstd[:, t:t + 1],
                                                      ALU.subtract, ALU.mult), m, xn_free[0])
        return r

    for n, e in engines.items():
        e.start_stage(sem(f"s_{n}_A"))
    sa = ExitStack()
    x0 = sb(sa, "x0", [P, B * TT, P])
    cT = sb(sa, "cT", [P, B])
    sig = sb(sa, "sig", [P, B])
    wmod = sb(sa, "wmod", [P, 6 * D])
    wdq = sb(sa, "wdq", [P, AQ])
    wdkv = sb(sa, "wdkv", [P, AQ])
    wq3 = sb(sa, "wq3", [AQ, 3, D])
    wuk = sb(sa, "wuk", [AQ, D])
    wk2 = sb(sa, "wk2", [P, 2, D])
    wuv = sb(sa, "wuv", [AQ, D])
    wo_a = sb(sa, "wo_a", [P, D])
    bv = sb(sa, "bv", [P, D])
    ropec = sb(sa, "ropec", [P, T])
    ropes = sb(sa, "ropes", [P, T])
    selg = sb(sa, "selg", [P, NG, P])
    msel = sb(sa, "msel", [AH, NG, P])
    onesel = sb(sa, "onesel", [1, P])
    ones = sb(sa, "ones", [1, T])
    lam = sb(sa, "lam", [P, 2])
    hT = sb(sa, "hT", [P, T])
    ctq = sb(sa, "ctq", [AQ, T])
    ctkv = sb(sa, "ctkv", [AQ, T])
    rot = sb(sa, "rot", [P, 3, T])
    qkT = sb(sa, "qkT", [P, 2, 2, T])
    hi = sb(sa, "hi", [P, T], F32R)
    q3 = sb(sa, "q3", [P, NG, T], F32R)
    k3 = sb(sa, "k3", [P, 2, NG, T], F32R)
    q3m = sb(sa, "q3m", [P, NG, T], F32R)
    vtok = sb(sa, "vtok", [P, 2, TT, AH, AD + 1])
    mx = sb(sa, "mx", [P, TT, AH])
    nmT = sb(sa, "nmT", [AH, T])
    pT = sb(sa, "pT", [P, 2, TT, T])
    rden = sb(sa, "rden", [P, TT, AH])
    otok = sb(sa, "otok", [P, TT, AH, AD])
    oT = sb(sa, "oT", [P, T])
    yT = sb(sa, "yT", [P, T])

    loads = [(x0[:, :, :], a["x"].rearrange("b (t p) d -> p (b t) d", p=P)),
             (cT[:, :], a["cT"]), (wmod[:, :], a["wmod"]), (wdq[:, :], a["wdq"]), (wdkv[:, :], a["wdkv"]),
             (wq3[:, :, :], a["wq3"].rearrange("w k n -> k w n")), (wuk[:, :], a["wuk"]),
             (wk2[:, :, :], a["wk2"].rearrange("w k n -> k w n")), (wuv[:, :], a["wuv"]),
             (wo_a[:, :], a["wo_a"]), (bv[:, :], a["bv"].rearrange("(o n) -> o n", o=1).broadcast_to([P, D])),
             (ropec[:, :], a["ropec"]), (ropes[:, :], a["ropes"]),
             (selg[:, :, :], a["selg"]), (msel[:, :, :], a["msel"]), (onesel[:, :], a["onesel"]),
             (ones[:, :], a["ones"]), (lam[:, :], a["lam"])]
    for dst, src in loads:
        sp.dma(lambda e, d=dst, s=src: e.dma_start(d, s), s_a)
    loaded = (s_a, 16 * len(loads))

    eps_set = pool.do(lambda e: e.memset(epsc[:, :], EPS))
    v_ones = pool.do(lambda e: e.memset(vtok[:, :, :, :, AD:AD + 1], 1.0))
    ring = Banks([bank(4), bank(5)])

    m = act.do(lambda e: e.activation(sig[:, :], cT[:, :], ACT.Exp, scale=-1.0), loaded)
    m = dve.do(lambda e: e.tensor_scalar(sig[:, :], sig[:, :], 1.0, None, ALU.add), m, loaded)
    m = dve.do(lambda e: e.reciprocal(sig[:, :], sig[:, :]), m)
    m = dve.do(lambda e: e.tensor_tensor(sig[:, :], sig[:, :], cT[:, :], ALU.mult), m)
    i, bk, _ = ring.take()
    for j in range(6):
        mm = pe.do(lambda e, j=j, bk=bk: e.matmul(bk[:, j * B:(j + 1) * B], wmod[:, j * D:(j + 1) * D], sig[:, :],
                                                  start=True, stop=True), m, loaded, signal=j == 5)
    mod_v = mod[:, :, :].rearrange("p j b -> p (j b)")
    m = dve.do(lambda e, bk=bk: e.tensor_copy(mod_v, bk[:, 0:6 * B]), mm)
    ring.free[i] = m
    gate, sgn, mag = mod[:, 2::3, :], rot[:, 0, 0:2 * B], rot[:, 1, 0:2 * B]
    sgn, mag = (v.rearrange("p (j b) -> p j b", b=B) for v in (sgn, mag))
    m = dve.do(lambda e: e.tensor_scalar(mod[:, 1::3, :], mod[:, 1::3, :], 1.0, None, ALU.add), m)
    m = dve.do(lambda e: e.tensor_scalar(sgn, gate, 0.0, 2.0, ALU.is_ge, ALU.mult), m)
    m = dve.do(lambda e: e.scalar_tensor_tensor(out=mag, in0=gate, scalar=-1.0, in1=gate, op0=ALU.mult,
                                                op1=ALU.max), m)
    m = dve.do(lambda e: e.tensor_scalar(mag, mag, 0.25, None, ALU.max), m)
    m = dve.do(lambda e: e.scalar_tensor_tensor(out=gate, in0=sgn, scalar=-1.0, in1=mag, op0=ALU.add,
                                                op1=ALU.mult), m)
    mod_ready = m

    q_free = [None, None]
    state = {}

    def prepare(b):
        par = b % 2
        x_tile = lambda t: x0[:, b * TT + t, :]
        i, bk, free = ring.take()
        m = transpose_tiles(bk, x_tile, after=[loaded, free])
        ring.free[i] = act.do(lambda e, bk=bk: e.copy(xT[:, b, :], bk), m)
        m = normalise(x_tile, loaded)
        i, bk, free = ring.take()
        m = transpose_tiles(bk, lambda t: xn[:, t, :], after=[m, free])
        xn_free[0] = m
        h = act.do(lambda e, bk=bk: e.activation(hT[:, :], bk, ACT.Identity, bias=mod[:, 0, b:b + 1],
                                          scale=mod[:, 1, b:b + 1]), m, mod_ready, state.get("h_read"))
        ring.free[i] = h
        ct = []
        for w, dst, key in ((wdq, ctq, "b_dq"), (wdkv, ctkv, "b_dkv")):
            i, bk, free = ring.take()
            m = pe.do(lambda e, w=w, bk=bk: e.matmul(bk[0:AQ, :], w[:, :], hT[:, :], start=True, stop=True),
                      h, free)
            m = act.do(lambda e, bk=bk, dst=dst, key=key: e.activation(dst[:, :], bk[0:AQ, :], ACT.Identity,
                                                                       bias=vec(key, AQ)), m,
                       state.get("ct_read"))
            ring.free[i] = m
            ct.append(m)
        for n, (names, ws, srcs) in enumerate((
                (("bq_c", "bq_r", "bq_s"), (wq3[:, 0, :], wq3[:, 1, :], wq3[:, 2, :]), (ctq, ctq, ctq)),
                (("bk_c", "bk_r", "bk_s"), (wuk[:, :], wk2[:, 0, :], wk2[:, 1, :]), (ctkv, hT, hT)))):
            r = []
            for j in (1, 2, 0):
                i, bk, free = ring.take()
                m = pe.do(lambda e, bk=bk, w=ws[j], s=srcs[j]: e.matmul(bk, w, s[:, :], start=True, stop=True),
                          ct, free)
                if j:
                    tab = ropec if j == 1 else ropes
                    m = dve.do(lambda e, bk=bk, j=j, tab=tab, key=names[j]: e.scalar_tensor_tensor(
                        out=rot[:, j, :], in0=bk, scalar=vec(key), in1=tab[:, :], op0=ALU.add, op1=ALU.mult),
                        m, dve.last())
                else:
                    m = dve.do(lambda e, bk=bk, key=names[0]: e.scalar_tensor_tensor(
                        out=rot[:, 0, :], in0=bk, scalar=vec(key), in1=rot[:, 1, :], op0=ALU.add, op1=ALU.add),
                        m, r)
                ring.free[i] = m
                r.append(m)
            state["qk", par, n] = dve.do(lambda e, n=n: e.tensor_tensor(qkT[:, par, n, :], rot[:, 0, :],
                                                                        rot[:, 2, :], ALU.add), r, q_free[par])
        i, bk, free = ring.take()
        for t in range(TT):
            m = pe.do(lambda e, t=t, bk=bk: e.matmul(bk[:, t * P:(t + 1) * P], ctkv[:, t * P:(t + 1) * P],
                                                     wuv[:, :], start=True, stop=True), free, signal=t == TT - 1)
        state["ct_read"] = state["h_read"] = m
        bv_all = bv[:, :].rearrange("p (o h d) -> p o h d", o=1, h=AH).broadcast_to([P, TT, AH, AD])
        m = dve.do(lambda e, bk=bk: e.tensor_tensor(
            vtok[:, par, :, :, 0:AD], bk.rearrange("p (t h d) -> p t h d", t=TT, h=AH), bv_all, ALU.add),
            m, v_ones, state.get(("v_read", par)))
        ring.free[i] = state["v", par] = m
        for g in range(NG):
            pack(q3[:, g, :], par, 0, g, [], state.get("q3_read"))
            state["packed", par, g] = pack(k3[:, par, g, :], par, 1, g, [(onesel[:, :], ones[:, :])],
                                           state.get(("k3_read", par)))

    def pack(dst, par, n, g, extra, free_dst, *after):
        i, bk, free = ring.take()
        m = pe.do(lambda e: e.matmul(bk, selg[:, g, :], qkT[:, par, n, :], start=True, stop=not extra),
                  state["qk", par, n], free, signal=not extra)
        for lhsT, rhs in extra:
            m = pe.do(lambda e, lhsT=lhsT, rhs=rhs: e.matmul(bk, lhsT, rhs, start=False, stop=True), after)
        h = act.do(lambda e: e.copy(hi[:, :], bk), m, state.get("hi_read"))
        m = dve.do(lambda e: e.scalar_tensor_tensor(out=dst, in0=hi[:, :].bitcast(F32), scalar=lam[:, n:n + 1],
                                                    in1=bk, op0=ALU.mult, op1=ALU.add), h, free_dst)
        state["hi_read"] = m
        ring.free[i] = m
        return m

    def maxima(b, h):
        par, g, r = b % 2, h // AG, 32 * (h % AG)
        for t in range(TT):
            i, bk, free = ring.take()
            m = pe.do(lambda e, t=t, bk=bk: e.matmul(bk, q3[r:r + 32, g, t * P:(t + 1) * P], k3[r:r + 32, par, g, :],
                                                     start=True, stop=True), state["packed", par, g], free)
            ring.free[i] = dve.do(lambda e, t=t, bk=bk: e.tensor_reduce(mx[:, t, h:h + 1], bk, AX_X, ALU.max),
                                  m, state.get("mx_read"))
        if h == AH - 1:
            state["q3_read"] = m

    def spread_maxima(b):
        par = b % 2
        i, bk, free = ring.take()
        for t in range(TT):
            m = pe.do(lambda e, t=t: e.transpose(bk[0:AH, t * P:(t + 1) * P], mx[:, t, :], ident[:, :]),
                      dve.last(), free, signal=t == TT - 1)
        state["mx_read"] = m
        m = ring.free[i] = act.do(lambda e: e.mul(nmT[:, :], bk[0:AH, :], -1.0), m, state.get("nm_read"))
        for g in range(NG):
            state["packed_m", g] = pack(q3m[:, g, :], par, 0, g, [(msel[:, g, :], nmT[:, :])],
                                        state.get("q3m_read"), m)
        state["nm_read"] = pe.last()
        q_free[par] = pe.last()

    score_free = [None, None]
    pT_free = [None, None]
    exps = {}

    def exponentials(b, h):
        par, g, r = b % 2, h // AG, 32 * (h % AG)
        for half in range(2):
            for c in range(2 * half, 2 * half + 2):
                m = pe.do(lambda e, c=c: e.matmul(bank(c), k3[r:r + 32, par, g, c * P:(c + 1) * P],
                                                  q3m[r:r + 32, g, :], start=True, stop=True),
                          state["packed_m", g], score_free[half], signal=c % 2 == 1)
            m = act.do(lambda e, half=half: e.activation(pT[:, h % 2, 2 * half:2 * half + 2, :],
                                                         psum[:, 2 * half:2 * half + 2, :], ACT.Exp,
                                                         scale=1.0 / float(np.sqrt(np.float32(AH + AQ + AQ)))),
                       m, pT_free[h % 2])
            score_free[half] = m
        exps[h] = m
        if h == AH - 1:
            state["k3_read", par] = state["q3m_read"] = pe.last()

    out_free = [None, None]
    HB = AH // 2

    def weighted(b, h):
        par, side, hh = b % 2, h // HB, h % HB
        o = bank(6 + side)[:, 0:TT * HB * (AD + 1)].rearrange("p (t h d) -> p t h d", t=TT, h=HB)
        for t in range(TT):
            for c in range(TT):
                m = pe.do(lambda e, t=t, c=c: e.matmul(o[:, t, hh, :], pT[:, h % 2, c, t * P:(t + 1) * P],
                                                       vtok[:, par, c, h, :], start=c == 0, stop=c == TT - 1),
                          exps[h], state["v", par], out_free[side] if hh == 0 else None,
                          signal=t == TT - 1 and c == TT - 1)
        pT_free[h % 2] = m
        if hh == HB - 1:
            hs = slice(side * HB, side * HB + HB)
            r = dve.do(lambda e: e.reciprocal(rden[:, :, hs], o[:, :, :, AD]), m)
            den = rden[:, :, hs].rearrange("p t (h o) -> p t h o", o=1).broadcast_to([P, TT, HB, AD])
            m = dve.do(lambda e: e.tensor_tensor(otok[:, :, hs, :], o[:, :, :, 0:AD], den, ALU.mult), r,
                       state.get("otok_read"))
            out_free[side] = m
        if h == AH - 1:
            state["v_read", par] = pe.last()
            state["otok"] = m

    def finish_attention(b):
        i, bk, free = ring.take()
        m = transpose_tiles(bk, lambda t: otok[:, t, :, :].rearrange("p h d -> p (h d)"), after=[state["otok"], free])
        state["otok_read"] = m
        m = ring.free[i] = act.do(lambda e, bk=bk: e.copy(oT[:, :], bk), m)
        i, bk, free = ring.take()
        m = pe.do(lambda e, bk=bk: e.matmul(bk, wo_a[:, :], oT[:, :], start=True, stop=True), m, free)
        m = ring.free[i] = dve.do(lambda e, bk=bk: e.tensor_scalar(yT[:, :], bk, vec("b_o"), mod[:, 2, b:b + 1],
                                                                   ALU.add, ALU.mult), m)
        m = dve.do(lambda e: e.tensor_tensor(xT[:, b, :], xT[:, b, :], yT[:, :], ALU.add), m, act.last())
        i, bk, free = ring.take()
        m = transpose_tiles(bk, lambda t: xT[:, b, t * P:(t + 1) * P], after=[m, free])
        m = ring.free[i] = normalise(lambda t, bk=bk: bk[:, t * P:(t + 1) * P], m)
        i, bk, free = ring.take()
        m = transpose_tiles(bk, lambda t: xn[:, t, :], after=[m, free])
        xn_free[0] = m
        ring.free[i] = act.do(lambda e, bk=bk: e.activation(rT[:, b, :], bk, ACT.Identity, bias=mod[:, 3, b:b + 1],
                                                            scale=mod[:, 4, b:b + 1]), m)

    prepare(0)
    for h in range(AH):
        maxima(0, h)
    for b in range(B):
        spread_maxima(b)
        if b + 1 < B:
            prepare(b + 1)
        for h in range(AH):
            exponentials(b, h)
            if b + 1 < B:
                maxima(b + 1, h)
            if h:
                weighted(b, h - 1)
        weighted(b, AH - 1)
        finish_attention(b)
    sa.close()

    ends = start_stage("B")
    identb = sb(ctx, "identb", [P, P], BF16)
    masks = sb(ctx, "masks", [P, 2, 512], BF16)
    tabs = sb(ctx, "tabs", [P, 4, T])
    pairsel = sb(ctx, "pairsel", [P, 2])
    WCH = WCOLS // 8
    w_raw = sb(ctx, "w_raw", [P, 2, WCH])
    w_hi = sb(ctx, "w_hi", [P, WCOLS], F32R)
    w_lo = sb(ctx, "w_lo", [P, WCOLS], F32R)
    wo = sb(ctx, "wo", [P, HP, D])
    w1_hi = sb(ctx, "w1_hi", [P, 2 * DI], F32R)
    w1_lo = sb(ctx, "w1_lo", [P, 2 * DI], F32R)
    w2 = sb(ctx, "w2", [P, NC, D])
    xs = sb(ctx, "xs", [P, WIN + T])
    xs_hi = sb(ctx, "xs_hi", [P, WIN + T], F32R)
    xs_lo = sb(ctx, "xs_lo", [P, WIN + T], F32R)
    t2 = sb(ctx, "t2", [P, 2, T])
    sq = sb(ctx, "sq", [P, 2, T])
    GT = 4
    u = sb(ctx, "u", [P, 2 * GT, T])
    rn = sb(ctx, "rn", [P, 2, TT, 2 * GT])
    rn2 = sb(ctx, "rn2", [P, TT, 4 * GT])
    rnT = sb(ctx, "rnT", [4 * GT, 2, T], F32R)
    selr = sb(ctx, "selr", [4 * GT, GT, P], F32R)
    qz = sb(ctx, "qz", [P, HP, NWIN, 2, WIN])
    kT = sb(ctx, "kT", [P, HP, WIN + T])
    v = sb(ctx, "v", [P, 2, H, DH + 1])
    smax = sb(ctx, "smax", [P, 2 * HP])
    sdiff = sb(ctx, "sdiff", [P, 2 * HP, 2 * WIN])
    px = sb(ctx, "px", [P, 2 * HP, P])
    pxT = sb(ctx, "pxT", [P, 2 * HP, P])
    rd = sb(ctx, "rd", [P, H])
    on = sb(ctx, "on", [P, H, DH])
    onT = sb(ctx, "onT", [P, HP, P])
    hn, gel, hid = u[:, 0, :], u[:, 1, :], u[:, 2:2 + NC, :]
    hn_hi, hn_lo = xs_hi[:, WIN:], xs_lo[:, WIN:]

    cb = [(u[:, 1:3, :], a["masks"]), (tabs[:, :, :], a["tabs"]),
          (pairsel[:, :], a["pairsel"]), (u[0:4 * GT, 0, :], a["selr"].rearrange("k g p -> k (g p)"))]
    s_cb = sem("s_cb")
    sp.wait(ends)
    for dst, src in cb:
        sp.dma(lambda e, d=dst, s=src: e.dma_start(d, s), s_cb)
    constb = (s_cb, 16 * len(cb))

    landed = [0, 0]
    raw_free = [None, None]

    def split(src, hi_, lo_, n, ready, free):
        for c in range(0, n, 512):
            s = slice(c, min(c + 512, n))
            m = pool.do(lambda e, s=s: e.tensor_copy(hi_[:, s], src[:, s]), ready, free)
            m = pool.do(lambda e, s=s: e.tensor_tensor(lo_[:, s], src[:, s], hi_[:, s].bitcast(F32), ALU.subtract), m)
        return m

    def split_columns(pieces, hi_, lo_, free):
        width = hi_.shape[1]
        for c0 in range(0, width, WCH):
            c1, half = min(c0 + WCH, width), state["half"]
            state["half"] = 1 - half
            for w, s0 in pieces:
                b0, b1 = max(c0, s0), min(c1, s0 + w.shape[1])
                if b0 < b1:
                    sp.dma(lambda e, w=w, half=half, s0=s0, b0=b0, b1=b1, c0=c0: e.dma_start(
                        w_raw[:, half, b0 - c0:b1 - c0], w[:, b0 - s0:b1 - s0]), s_wraw[half], raw_free[half])
                    landed[half] += 16
            m = split(w_raw[:, half, :], hi_[:, c0:c1], lo_[:, c0:c1], c1 - c0, (s_wraw[half], landed[half]), free)
            raw_free[half] = m
        return m

    def split_qkv(i, free):
        return split_columns([(a["wqkv"][i], 0), (a["wqks"][i], 3 * INNER)], w_hi, w_lo, free)

    def split_w1(i, free):
        return split_columns([(a["w1"][i], 0)], w1_hi, w1_lo, free)

    state["half"] = 0

    def load_rest(i, *after):
        sp.dma(lambda e: e.dma_start(wo[:, :, :], a["wo"][i].rearrange("(m p) d -> p m d", p=P)), s_wffn[i], after)
        for c, (c0, n) in enumerate(DI_CHUNKS):
            sp.dma(lambda e, c=c, c0=c0, n=n: e.dma_start(w2[0:n, c, :], a["w2"][i, c0:c0 + n, :]), s_wffn[i])

    REST = 16 * (1 + NC)
    load_rest(0)

    for t_ in (xs[:, 0:WIN + 1], xs_hi[:, 0:WIN], xs_lo[:, 0:WIN], qz[:, :, :, :, :], kT[:, :, 0:WIN], px[:, :, :]):
        pool.do(lambda e, t_=t_: e.memset(t_.bitcast(F32) if t_.dtype == F32R else t_, 0.0))
    zeroed = pool.do(lambda e: e.memset(v[:, :, :, DH:DH + 1], 1.0))
    selr_ready = pool.do(lambda e: e.tensor_copy(selr[:, :, :].rearrange("k g p -> k (g p)"), u[0:4 * GT, 0, :]), constb)
    pool.do(lambda e: e.tensor_copy(masks[:, :, :], u[:, 1:3, :]), constb)
    masks_ready = pool.do(lambda e: e.tensor_copy(identb[:, :], ident[:, :]), consts)

    def do_mm3(o, lhs, rhs, *after, signal=True):
        pe.do(lambda e: e.matmul(o, lhs[0], rhs[0], start=True, stop=False), *after, signal=False)
        pe.do(lambda e: e.matmul(o, lhs[0], rhs[1], start=False, stop=False), signal=False)
        return pe.do(lambda e: e.matmul(o, lhs[1], rhs[0], start=False, stop=True), signal=signal)

    st = {}

    def shift(b, ready, attention):
        free = [st.get("xs_read")]
        m1 = act.do(lambda e: e.copy(xs[0:64, WIN:WIN + T], rT[0:64, b, :]), ready, free, zeroed)
        m2 = act.do(lambda e: e.copy(xs[64:P, WIN + 1:WIN + T], rT[64:P, b, 0:T - 1]), ready, free, zeroed)
        if not attention:
            return m2
        h_ = act.do(lambda e: e.copy(xs_hi[:, WIN:], xs[:, WIN:]), m1, m2, st.get("xsp_read"))
        return dve.do(lambda e: e.tensor_tensor(xs_lo[:, WIN:], xs[:, WIN:], xs_hi[:, WIN:].bitcast(F32),
                                                ALU.subtract), h_)

    def project(i, b, ready):
        cols = lambda c: (w_hi[:, c:c + P], w_lo[:, c:c + P])
        x_ = (xs_hi[:, WIN:], xs_lo[:, WIN:])
        pairs = Banks([(bank(0), bank(1)), (bank(2), bank(3))])
        pairs.free = [[st.get("free01")], [st.get("free23")]]
        rbank = Banks([bank(5), bank(6)])
        rbank.free = [st.get("free5"), st.get("free6")]
        nbank_free = st.get("free4")
        tiles = [(which, m_) for which in (0, 1) for m_ in range(HP)]
        rnf = [st.get("rn_read0"), st.get("rn_read1")]
        uf = st.setdefault("u_free", [None] * (2 * GT))
        marks = {}

        def rotate(n):
            which, m_ = tiles[n]
            w0, ws = (WQ, WQS) if which == 0 else (WK, WKS)
            gain = ("qs", "qs_s") if which == 0 else ("ks", "ks_s")
            slot, j = n % (2 * GT), n % 2
            bi, (pa, pb), free = pairs.take()
            ma = do_mm3(pa, cols(w0 + m_ * P), x_, ready, free)
            mb = do_mm3(pb, cols(ws + m_ * P), x_)
            s_ = act.do(lambda e: e.activation(sq[:, j, :], pa, ACT.Square), ma, st.get(("sq_read", j)))
            a1 = dve.do(lambda e: e.scalar_tensor_tensor(out=u[:, slot, :], in0=pa, scalar=vec((gain[0], i)),
                                                         in1=tabs[:, 2 * which, :], op0=ALU.mult, op1=ALU.mult),
                        ma, s_, constb, uf[slot])
            a2 = dve.do(lambda e: e.scalar_tensor_tensor(out=t2[:, j, :], in0=pb, scalar=vec((gain[1], i)),
                                                         in1=tabs[:, 2 * which + 1, :], op0=ALU.mult, op1=ALU.mult),
                        mb, st.get(("t_read", j)))
            pairs.free[bi] = a2
            m = pool.do(lambda e: e.tensor_tensor(u[:, slot, :], u[:, slot, :], t2[:, j, :], ALU.add), a2)
            st["t_read", j] = m
            marks["u", n] = m
            g2, k = (n // GT) % 2, n % GT
            for t in range(TT):
                o = bank(4)[:, (g2 * TT + t) * 2 * GT + 2 * k:][:, 0:2]
                m = pe.do(lambda e, t=t, o=o: e.matmul(o, sq[:, j, t * P:(t + 1) * P], pairsel[:, :], start=True,
                                                       stop=True), s_, constb, nbank_free, marks.get(("n_read", n // GT - 1)),
                          signal=t == TT - 1)
            st["sq_read", j] = m
            marks["sum", n] = m

        def norms(g):
            g2 = g % 2
            src = bank(4)[:, g2 * TT * 2 * GT:(g2 + 1) * TT * 2 * GT]
            r = rn[:, g2, :, :].rearrange("p t h -> p (t h)")
            m = dve.do(lambda e: e.tensor_scalar(r, src, 1e-24, None, ALU.max), marks["sum", g * GT + GT - 1], rnf[g2])
            marks["n_read", g] = m
            m = act.do(lambda e: e.activation(r, r, ACT.Sqrt), m)
            m = dve.do(lambda e: e.reciprocal(r, r), m)
            r_hi, r_lo = rn2[:, :, 0:2 * GT], rn2[:, :, 2 * GT:]
            m = dve.do(lambda e: e.tensor_copy(r_hi.bitcast(F32R), rn[:, g2, :, :]), m, st.get("rn2_read"))
            m = dve.do(lambda e: e.tensor_tensor(r_lo, rn[:, g2, :, :], r_hi, ALU.subtract), m)
            rnf[g2] = m
            bi, rb, free = rbank.take()
            for t in range(TT):
                m = pe.do(lambda e, t=t: e.transpose(rb[0:4 * GT, t * P:(t + 1) * P], rn2[:, t, :], ident[:, :]),
                          m, free, signal=t == TT - 1) or m
            st["rn2_read"] = m
            marks["rn", g] = rbank.free[bi] = act.do(lambda e: e.copy(rnT[:, g2, :], rb[0:4 * GT, :]), m,
                                                     st.get(("rnT_read", g2)))

        def scale(n):
            which, m_ = tiles[n]
            g, k, slot = n // GT, n % GT, n % (2 * GT)
            g2 = g % 2
            bi, rb, free = rbank.take()
            m = pe.do(lambda e: e.matmul(rb, selr[:, k, :], rnT[:, g2, :], start=True, stop=True),
                      marks["rn", g], free, selr_ready)
            st["rnT_read", g2] = m
            if which == 0:
                for hp in range(2):
                    s_ = slice(64 * hp, 64 * hp + 64)
                    m2 = dve.do(lambda e, s_=s_, hp=hp: e.tensor_tensor(
                        qz[s_, m_, :, hp, :], u[s_, slot, :].rearrange("p (w q) -> p w q", q=WIN),
                        rb[s_, :].rearrange("p (w q) -> p w q", q=WIN), ALU.mult), m, marks["u", n], zeroed,
                                st.get("qk_read"))
            else:
                m2 = dve.do(lambda e: e.tensor_tensor(kT[:, m_, WIN:], u[:, slot, :], rb, ALU.mult), m,
                            marks["u", n], zeroed, st.get("qk_read"))
            rbank.free[bi] = uf[slot] = m2
            return m2

        NT = len(tiles)
        for n in range(NT + GT + 1):
            if n < NT:
                rotate(n)
            if n % GT == GT - 1 and n < NT:
                norms(n // GT)
            if n >= GT + 1:
                m = scale(n - GT - 1)
        st["free01"], st["free23"] = pairs.free
        st["free5"], st["free6"] = rbank.free
        st["free4"] = marks["n_read", NT // GT - 1]
        st["rn_read0"], st["rn_read1"] = rnf
        st["qk"] = m

    def attend(i, b, ready, wo_ready):
        bfree = {k: [st.get(k)] for k in ("free01", "free23", "free4", "free5", "free6")}
        pring = Banks([bank(2), bank(3)])
        pring.free = [bfree["free23"], bfree["free23"]]
        s_free = [bfree["free01"]]
        o_free = [[bfree["free4"], bfree["free5"], bfree["free6"]]]
        y_free = [st.get("free7")]
        HPB = [(0, 6), (6, 11), (11, 16)]
        mk = {}

        def scores(t):
            first = 1 if t == 0 else 0
            for half in range(2):
                pe.do(lambda e, half=half: e.matmul(bank(half), identb[:, :], masks[:, first, :], start=True, stop=False,
                                                    skip_group_check=True), s_free[0], masks_ready, st["qk"], signal=False)
                for m_ in range(half * HP // 2, (half + 1) * HP // 2):
                    for s_ in range(2):
                        for w_ in range(2):
                            win = 4 * t + 2 * w_ + s_
                            o = bank(half)[64 * w_:64 * w_ + 64, ((m_ % (HP // 2)) * 2 + s_) * 64:][:, 0:64]
                            last = m_ % (HP // 2) == HP // 2 - 1 and s_ == 1 and w_ == 1
                            m = pe.do(lambda e, o=o, m_=m_, win=win, last=last: e.matmul(
                                o, qz[:, m_, win, :, :].rearrange("p h q -> p (h q)"), kT[:, m_, win * WIN:(win + 2) * WIN],
                                start=False, stop=last, skip_group_check=True), signal=last and half == 1)
            sv = psum[:, 0:2, :].rearrange("p a (k j) -> p (a k) j", j=2 * WIN)
            m = dve.do(lambda e: e.tensor_reduce(smax[:, :], sv, AX_X, ALU.max), m)
            mb = smax[:, :].rearrange("p (k o) -> p k o", o=1).broadcast_to([P, 2 * HP, 2 * WIN])
            m = dve.do(lambda e: e.tensor_tensor(sdiff[:, :, :], sv, mb, ALU.subtract), m, st.get("sdiff_read"))
            s_free[0] = m
            for w_ in range(2):
                r = slice(64 * w_, 64 * w_ + 64)
                m2 = act.do(lambda e, r=r: e.activation(px[r, :, r], sdiff[r, :, :], ACT.Exp, scale=8.0), m,
                            st.get("px_read"), zeroed)
            st["sdiff_read"] = m2
            mk["px", t] = m2

        def values(t):
            for s_ in range(2):
                c0 = t * P + s_ * WIN
                for half in range(2):
                    bi, bk, free = pring.take()
                    x_ = (xs_hi[:, c0:c0 + P], xs_lo[:, c0:c0 + P])
                    wc = WV + half * 512
                    m = do_mm3(bk, x_, (w_hi[:, wc:wc + 512], w_lo[:, wc:wc + 512]), ready, free)
                    hs = slice(half * 8, half * 8 + 8)
                    m = act.do(lambda e, bk=bk, hs=hs, s_=s_: e.copy(
                        v[:, s_, hs, 0:DH], bk.rearrange("p (h d) -> p h d", d=DH)), m, zeroed, st.get("v_read"))
                    pring.free[bi] = m
            mk["v", t] = m

        def transposes(t):
            for q in range(4):
                bi, bk, free = pring.take()
                for k in range(4):
                    m = pe.do(lambda e, k=k, q=q, bk=bk: e.transpose(bk[:, k * P:(k + 1) * P], px[:, 4 * q + k, :], ident[:, :]),
                              mk["px", t], free, signal=k == 3)
                eng = act if q % 2 == 0 else dve
                for hp in range(2):
                    dst = pxT[:, 4 * q:4 * q + 4, hp * 64:hp * 64 + 64].rearrange("p k (w q) -> p k w q", w=2)
                    src = bk.rearrange("p (k w h q) -> p k w h q", w=2, h=2, q=WIN)[:, :, :, hp, :]
                    f = (lambda e, dst=dst, src=src: e.copy(dst, src)) if eng is act else \
                        (lambda e, dst=dst, src=src: e.tensor_copy(dst, src))
                    m2 = eng.do(f, m, st.get("pxT_read"))
                mk["pxT", t, q] = pring.free[bi] = m2
            st["px_read"] = m

        def apply(t):
            for g, (h0, h1) in enumerate(HPB):
                bk = bank(4 + g)
                for h in range(h0, h1):
                    m_, hp = divmod(h, 2)
                    for s_ in range(2):
                        lhs = pxT[:, 2 * m_ + s_, hp * 64:hp * 64 + 64]
                        o = bk[64 * s_:64 * s_ + 64, (h - h0) * (DH + 1):(h - h0 + 1) * (DH + 1)]
                        m = pe.do(lambda e, o=o, lhs=lhs, h=h, s_=s_: e.matmul(o, lhs, v[:, s_, h, :], start=True,
                                                                              stop=True),
                                  mk["pxT", t, (2 * m_ + s_) // 4], mk["v", t], o_free[0],
                                  signal=h == h1 - 1 and s_ == 1)
                ov = bk[:, 0:(h1 - h0) * (DH + 1)].rearrange("p (h d) -> p h d", d=DH + 1)
                r = dve.do(lambda e, ov=ov, h0=h0, h1=h1: e.reciprocal(rd[:, h0:h1], ov[:, :, DH]), m)
                den = rd[:, h0:h1].rearrange("p (h o) -> p h o", o=1).broadcast_to([P, h1 - h0, DH])
                mk["on", g] = dve.do(lambda e, ov=ov, den=den, h0=h0, h1=h1: e.tensor_tensor(
                    on[:, h0:h1, :], ov[:, :, 0:DH], den, ALU.mult), r, st.get("on_read"))
            o_free[0] = mk["on", 2]
            st["v_read"] = st["pxT_read"] = m

        def output(t):
            for half in range(2):
                bi, bk, free = pring.take()
                for k in range(4):
                    c = 2 * (4 * half + k)
                    m = pe.do(lambda e, c=c, k=k, bk=bk: e.transpose(bk[:, k * P:(k + 1) * P], on[:, c:c + 2, :].rearrange("p h d -> p (h d)"),
                                                                     ident[:, :]), mk["on", 2], free, signal=k == 3)
                for k in range(4):
                    dst = onT[:, 4 * half + k, :].rearrange("p (w s q) -> p s w q", w=2, s=2)
                    srcv = bk[:, k * P:(k + 1) * P].rearrange("p (s w q) -> p s w q", w=2, s=2)
                    m2 = act.do(lambda e, dst=dst, srcv=srcv: e.copy(dst, srcv), m, st.get("onT_read"))
                pring.free[bi] = m2
            st["on_read"] = m
            for m_ in range(HP):
                m = pe.do(lambda e, m_=m_: e.matmul(bank(7)[:, t * P:(t + 1) * P], wo[:, m_, :], onT[:, m_, :],
                                                    start=m_ == 0, stop=m_ == HP - 1), m2, y_free[0], wo_ready,
                          signal=m_ == HP - 1)
            st["onT_read"] = m
            mk["y"] = m

        scores(0)
        values(0)
        for t in range(TT):
            transposes(t)
            if t + 1 < TT:
                scores(t + 1)
            apply(t)
            if t + 1 < TT:
                values(t + 1)
            output(t)
        st["xsp_read"] = st["qk_read"] = pe.last()
        m = dve.do(lambda e: e.tensor_tensor(rT[:, b, :], bank(7), rT[:, b, :], ALU.add), mk["y"])
        st["free7"] = m
        st["free01"] = s_free[0]
        st["free23"] = list(pring.free)
        st["free4"] = st["free5"] = st["free6"] = o_free[0]
        return m

    def feed_forward(i, b, ready, w_ready, w1_ready):
        m = shift(b, ready, False)
        m = transpose_tiles(bank(7), lambda t: xs[:, WIN + t * P:WIN + (t + 1) * P], after=[m, st["free7"]])
        st["xs_read"] = m
        m = normalise(lambda t: bank(7)[:, t * P:(t + 1) * P], m)
        m = transpose_tiles(bank(7), lambda t: xn[:, t, :], after=[m])
        xn_free[0] = m
        m = act.do(lambda e: e.activation(hn, bank(7), ACT.Identity, bias=vec(("b", i)), scale=vec(("g", i))),
                   m, st.get("hn_read"))
        st["free7"] = m
        h_ = act.do(lambda e: e.copy(hn_hi, hn), m, st.get("hns_read"))
        m = dve.do(lambda e: e.tensor_tensor(hn_lo, hn, hn_hi.bitcast(F32), ALU.subtract), h_,
                   st.get("hns_read"))
        st["hn_read"] = m
        x_ = (hn_hi, hn_lo)
        frees = [st["free01"], st["free23"]]
        for c, (c0, n) in enumerate(DI_CHUNKS):
            pa, pg = bank(2 * (c % 2)), bank(2 * (c % 2) + 1)
            mg = do_mm3(pg[0:n, :], (w1_hi[:, DI + c0:DI + c0 + n], w1_lo[:, DI + c0:DI + c0 + n]), x_, m,
                        frees[c % 2], w1_ready)
            ma = do_mm3(pa[0:n, :], (w1_hi[:, c0:c0 + n], w1_lo[:, c0:c0 + n]), x_)
            g_ = act.do(lambda e, pg=pg, n=n, c=c: e.activation(gel[0:n, :], pg[0:n, :], ACT.Gelu,
                                                                bias=vec(("b1g", i, c), n)), mg, st.get("gel_read"))
            h_ = dve.do(lambda e, pa=pa, n=n, c=c: e.scalar_tensor_tensor(
                out=hid[0:n, c, :], in0=pa[0:n, :], scalar=vec(("b1a", i, c), n), in1=gel[0:n, :], op0=ALU.add,
                op1=ALU.mult), ma, g_, st.get("hid_read"))
            frees[c % 2] = st["gel_read"] = h_
        st["hns_read"] = ma
        st["free01"], st["free23"] = frees
        for c, (c0, n) in enumerate(DI_CHUNKS):
            m = pe.do(lambda e, c=c, n=n: e.matmul(bank(7), w2[0:n, c, :], hid[0:n, c, :], start=c == 0,
                                                   stop=c == NC - 1), h_, st["free7"], w_ready, signal=c == NC - 1)
        st["hid_read"] = m
        m = dve.do(lambda e: e.scalar_tensor_tensor(out=rT[:, b, :], in0=bank(7), scalar=vec(("b2", i)),
                                                    in1=rT[:, b, :], op0=ALU.add, op1=ALU.add), m)
        st["free7"] = m
        return m

    res = [None] * B
    split_qkv(0, None)
    split_w1(0, None)
    for i in range(DEPTH):
        start_stage(f"layer{i}")
        st.clear()
        xn_free[0] = None
        res = [None] * B
        for b in range(B):
            ready = shift(b, None, True)
            st["xs_read"] = ready
            project(i, b, ready)
            res[b] = attend(i, b, ready, (s_wffn[i], REST))
        if i + 1 < DEPTH:
            split_qkv(i + 1, pe.last())
        for b in range(B):
            res[b] = feed_forward(i, b, res[b], (s_wffn[i], REST), None)
        if i + 1 < DEPTH:
            load_rest(i + 1, pe.last())
            split_w1(i + 1, pe.last())

    fin = sdiff[:, 0:8, :].rearrange("p k j -> p (k j)")
    ft = xn
    prev = None
    for b in range(B):
        m = dve.do(lambda e, b=b: e.scalar_tensor_tensor(out=xT[:, b, :], in0=rT[:, b, :], scalar=mod[:, 5, b:b + 1],
                                                         in1=xT[:, b, :], op0=ALU.mult, op1=ALU.add), res[b])
        m = transpose_tiles(bank(b), lambda t, b=b: xT[:, b, t * P:(t + 1) * P],
                            after=[m, st["free01"], st["free23"]])
        dst = px[:, 4 * b:4 * b + 4, :]
        m = act.do(lambda e, b=b, dst=dst: e.copy(dst.rearrange("p t d -> p (t d)"), bank(b)), m)
        sp.dma(lambda e, b=b, dst=dst: e.dma_start(out[b].rearrange("(t p) d -> p t d", p=P), dst), s_out, m)
    sp.wait((s_out, 16 * B))

    block = ctx.enter_context(nc.Block())

    def run(steps):
        def body(e):
            for step in steps:
                step(e)
        return body

    block.tensor(run(pe.steps))
    block.vector(run(dve.steps))
    block.scalar(run(act.steps))
    block.gpsimd(run(pool.steps))
    block.sync(run(sp.steps))
    ctx.close()


def constants():
    f = np.float32
    c = {"ident": np.eye(P, dtype=f)}
    pos = np.arange(T, dtype=f)[:, None]
    ids = np.arange(D // 2, dtype=f)
    theta = (f(10000.0) ** (f(-2.0) * ids) / f(D // 2)).astype(f)
    r = (pos * theta[None, :]).astype(f)
    c["ropec"] = np.ascontiguousarray(np.repeat(np.cos(r), 2, axis=1).T)
    sgn = np.where(np.arange(D) % 2 == 0, -1, 1).astype(f)
    c["ropes"] = np.ascontiguousarray(np.repeat(np.sin(r), 2, axis=1).T * sgn[:, None])
    selg, msel, onesel = np.zeros((P, NG, P), f), np.zeros((AH, NG, P), f), np.zeros((1, P), f)
    lam = np.zeros((P, 2), f)
    for g in range(NG):
        for h in range(AG):
            for k in range(3):
                for d in range(AD):
                    selg[(AG * g + h) * AD + d, g, 32 * h + AD * k + d] = 1
            msel[AG * g + h, g, 32 * h + 3 * AD] = 1
    for h in range(AG):
        onesel[0, 32 * h + 3 * AD] = 1
        lam[32 * h + 2 * AD:32 * h + 3 * AD, 0] = -1
        lam[32 * h + AD:32 * h + 2 * AD, 1] = -1
    c.update(selg=selg, msel=msel, onesel=onesel, lam=lam, ones=np.ones((1, T), f))
    half = np.arange(0, DH, 2, dtype=f)
    inv_freq = (f(1.0) / f(10000.0) ** (half / f(DH))).astype(f)
    t = np.arange(T, dtype=f)
    fr = (t[:, None] * inv_freq[None, :]).astype(f)
    fr = np.concatenate([fr, fr], -1)
    base = ((half + f(0.4 * DH)) / f(1.4 * DH)).astype(f)
    power = ((t - T // 2) / f(WIN // 2)).astype(f)
    sc = (base[None, :] ** power[:, None]).astype(f)
    sc = np.concatenate([sc, sc], -1)
    inv = (f(1.0) / sc).astype(f)
    s2 = np.where(np.arange(DH) < DH // 2, -1, 1).astype(f)
    two = lambda z: np.tile(z.astype(f).T, (2, 1))
    c["tabs"] = np.ascontiguousarray(np.stack([two(np.cos(fr) * sc), two(np.sin(fr) * sc * s2),
                                               two(np.cos(fr) * inv), two(np.sin(fr) * inv * s2)], axis=1))
    pairsel = np.zeros((P, 2), f)
    pairsel[0:64, 0] = 1
    pairsel[64:, 1] = 1
    c["pairsel"] = pairsel
    selr = np.zeros((16, 4, P), f)
    for k in range(4):
        for hp in range(2):
            for part in range(2):
                selr[8 * part + 2 * k + hp, k, 64 * hp:64 * hp + 64] = 1
    c["selr"] = selr
    q, j = np.arange(WIN)[:, None], np.arange(2 * WIN)[None, :]
    ok = (j >= q) & (j <= q + WIN)
    masks = np.zeros((P, 2, 4, 2, 2 * WIN), f)
    masks[:] = np.where(np.tile(ok, (4, 1)), 0.0, NEG)[:, None, None, None, :]
    masks[0:64, 1, :, 0, 0:WIN] = NEG
    c["masks"] = masks.reshape(P, 2, 512)
    return c


def kernel(**inputs):
    import concourse.bacc as bacc
    from concourse.bass_utils import run_bass_kernel_spmd

    x = {k.replace("L0_", ""): np.ascontiguousarray(v) for k, v in inputs.items()}
    pair = np.arange(D).reshape(-1, 2)[:, ::-1].reshape(-1)
    half = np.arange(DH).reshape(2, -1)[::-1].reshape(-1)
    swap = (np.arange(2 * H)[:, None] * DH + half[None, :]).reshape(-1)
    arrays = constants()
    vecs = np.zeros((P, NVEC), np.float32)

    def put(key, v):
        vecs[0:len(v), VEC[key]] = v

    put("bq_c", x["attn_Wu_q_b"])
    put("bq_r", x["attn_Wq_r_b"])
    put("bq_s", x["attn_Wq_r_b"][pair])
    put("bk_c", x["attn_Wu_k_b"])
    put("bk_r", x["attn_Wk_r_b"])
    put("bk_s", x["attn_Wk_r_b"][pair])
    put("b_o", x["attn_Wo_b"])
    put("b_dq", x["attn_Wd_q_b"])
    put("b_dkv", x["attn_Wd_kv_b"])
    for i in range(DEPTH):
        for key, v in (("qs", x["ffn_q_scale"][i]), ("ks", x["ffn_k_scale"][i])):
            put((key, i), np.concatenate([v, v]))
            put((key + "_s", i), np.concatenate([v[half], v[half]]))
        put(("g", i), x["ffn_ln_g"][i])
        put(("b", i), x["ffn_ln_b"][i])
        put(("b2", i), x["ffn_b2"][i])
        for c, (c0, n) in enumerate(DI_CHUNKS):
            put(("b1a", i, c), x["ffn_b1"][i, c0:c0 + n])
            put(("b1g", i, c), x["ffn_b1"][i, DI + c0:DI + c0 + n])
    arrays.update(
        vecs=vecs, x=x["attn_x"], cT=np.ascontiguousarray(x["c"].T), wmod=x["wmod"], wdq=x["attn_Wd_q_w"],
        wdkv=x["attn_Wd_kv_w"],
        wq3=np.stack([x["attn_Wu_q_w"], x["attn_Wq_r_w"], x["attn_Wq_r_w"][:, pair]]),
        wuk=x["attn_Wu_k_w"], wk2=np.stack([x["attn_Wk_r_w"], x["attn_Wk_r_w"][:, pair]]),
        wuv=x["attn_Wu_v_w"], wo_a=x["attn_Wo_w"], bv=x["attn_Wu_v_b"],
        wqkv=x["ffn_Wqkv"], wqks=np.ascontiguousarray(x["ffn_Wqkv"][:, :, swap]), wo=x["ffn_Wo"], w1=x["ffn_W1"],
        w2=x["ffn_W2"])
    nc = bacc.Bacc("TRN2", target_bir_lowering=False, num_devices=1)
    aps = {n: nc.dram_tensor(f"in_{n}", v.shape, mybir.dt.from_np(v.dtype), kind="ExternalInput").ap()
           for n, v in arrays.items()}
    out = nc.dram_tensor("out_x", (B, T, D), F32, kind="ExternalOutput").ap()
    build(nc, aps, out)
    r = run_bass_kernel_spmd(nc, [{f"in_{n}": v for n, v in arrays.items()}], core_ids=[0])
    return r.results[0]["out_x"]
```

```python
from contextlib import ExitStack

import numpy as np
import concourse.bass as bass
from concourse import mybir

F32 = mybir.dt.float32
F32R = mybir.dt.float32r
BF16 = mybir.dt.bfloat16
ALU = mybir.AluOpType
ACT = mybir.ActivationFunctionType
AX_X = mybir.AxisListType.X

P = 128
B, T, D = 4, 512, 128
TT = T // P
AH, AD = 16, 8
AQ = 64
AG = 4
NG = AH // AG
DEPTH, H, DH, WIN = 6, 16, 64, 32
INNER = H * DH
HP = H // 2
NWIN = T // WIN
DI = int(D * 4 * 2 / 3)
DI_CHUNKS = [(c, min(P, DI - c)) for c in range(0, DI, P)]
NC = len(DI_CHUNKS)
EPS = 1e-5
NEG = -1e30


VEC = {}
for _n in ("bq_c", "bq_r", "bq_s", "bk_c", "bk_r", "bk_s", "b_o", "b_dq", "b_dkv"):
    VEC[_n] = len(VEC)
for _i in range(DEPTH):
    for _n in ("qs", "ks", "g", "b", "b2"):
        VEC[_n, _i] = len(VEC)
    for _c in range(NC):
        VEC["b1a", _i, _c] = len(VEC)
        VEC["b1g", _i, _c] = len(VEC)
NVEC = len(VEC)


class Engine:

    def __init__(self):
        self.steps, self.sem, self.count, self.waited = [], None, 0, {}

    def start_stage(self, sem):
        self.sem, self.count = sem, 0

    def wait(self, *marks):
        for m in marks:
            if isinstance(m, (list, tuple)) and m and isinstance(m[0], (list, tuple, type(None))):
                self.wait(*m)
            elif m:
                sem, value = m
                if self.waited.get(sem.name, 0) < value:
                    self.waited[sem.name] = value
                    self.steps.append(lambda e, s=sem, v=value: e.wait_ge(s, v))

    def do(self, fn, *after, signal=True):
        self.wait(*after)
        if not signal:
            self.steps.append(fn)
            return None
        self.count += 1
        sem = self.sem
        self.steps.append(lambda e: fn(e).then_inc(sem, 1))
        return (sem, self.count)

    def dma(self, fn, sem, *after):
        self.wait(*after)
        self.steps.append(lambda e: fn(e).then_inc(sem, 16))

    def last(self):
        return (self.sem, self.count) if self.count else None


class Banks:

    def __init__(self, banks):
        self.banks, self.free, self.at = banks, [None] * len(banks), 0

    def take(self):
        i = self.at % len(self.banks)
        self.at += 1
        return i, self.banks[i], self.free[i]


def build(nc, a, out):
    ctx = ExitStack()
    sem = lambda name: ctx.enter_context(nc.semaphore(name))

    def sb(scope, name, shape, dt=F32):
        return scope.enter_context(nc.sbuf_tensor(name, shape, dt))

    pe, dve, act, pool, sp = (Engine() for _ in range(5))
    engines = {"pe": pe, "dve": dve, "act": act, "pool": pool}

    def start_stage(n):
        ends = [e.last() for e in engines.values()]
        for name, e in engines.items():
            e.start_stage(sem(f"s_{name}_{n}"))
        for e in engines.values():
            e.wait(ends)
        return ends

    psum = ctx.enter_context(nc.psum_tensor("psum", [P, 8, 512], F32))
    bank = lambda i: psum[:, i, :]

    ident = sb(ctx, "ident", [P, P])
    vecs = sb(ctx, "vecs", [P, NVEC])
    xT = sb(ctx, "xT", [P, B, T])
    rT = sb(ctx, "rT", [P, B, T])
    mod = sb(ctx, "mod", [P, 6, B])
    stats = sb(ctx, "stats", [P, TT, 6])
    mv = sb(ctx, "mv", [P, TT, 2])
    rstd = sb(ctx, "rstd", [P, TT])
    epsc = sb(ctx, "epsc", [P, 1])
    xn = sb(ctx, "xn", [P, TT, P])

    s_const, s_a, s_out = sem("s_const"), sem("s_a"), sem("s_out")
    s_wraw = [sem("s_wraw0"), sem("s_wraw1")]
    s_wo = [sem("s_wo0"), sem("s_wo1")]
    s_w2 = sem("s_w2")
    vec = lambda key, n=P: vecs[0:n, VEC[key]:VEC[key] + 1]

    sp.dma(lambda e: e.dma_start(ident[:, :], a["ident"]), s_const)
    sp.dma(lambda e: e.dma_start(vecs[:, :], a["vecs"]), s_const)
    consts = (s_const, 32)

    def transpose_tiles(bank_out, src, n_part=P, after=()):
        for t in range(TT):
            m = pe.do(lambda e, t=t: e.transpose(bank_out[:, t * P:(t + 1) * P], src(t), ident[:, :]),
                      after, consts, signal=t == TT - 1)
        return m

    xn_free = [None]

    def normalise(src, ready):
        for t in range(TT):
            m = dve.do(lambda e, t=t: e.bn_stats(stats[:, t, :], src(t)), ready, dve.last())
        for t in range(TT):
            m2 = dve.do(lambda e, t=t: e.bn_aggr(mv[:, t, :], stats[:, t, :]), m)
        m = act.do(lambda e: e.activation(rstd[:, :], mv[:, :, 1], ACT.Sqrt, bias=epsc[:, 0:1]), m2, eps_set)
        m = dve.do(lambda e: e.reciprocal(rstd[:, :], rstd[:, :]), m)
        for t in range(TT):
            r = dve.do(lambda e, t=t: e.tensor_scalar(xn[:, t, :], src(t), mv[:, t, 0:1], rstd[:, t:t + 1],
                                                      ALU.subtract, ALU.mult), m, xn_free[0])
        return r

    for n, e in engines.items():
        e.start_stage(sem(f"s_{n}_A"))
    sa = ExitStack()
    x0 = sb(sa, "x0", [P, B * TT, P])
    cT = sb(sa, "cT", [P, B])
    sig = sb(sa, "sig", [P, B])
    wmod = sb(sa, "wmod", [P, 6 * D])
    wdq = sb(sa, "wdq", [P, AQ])
    wdkv = sb(sa, "wdkv", [P, AQ])
    wq3 = sb(sa, "wq3", [AQ, 3, D])
    wuk = sb(sa, "wuk", [AQ, D])
    wk2 = sb(sa, "wk2", [P, 2, D])
    wuv = sb(sa, "wuv", [AQ, D])
    wo_a = sb(sa, "wo_a", [P, D])
    bv = sb(sa, "bv", [P, D])
    ropec = sb(sa, "ropec", [P, T])
    ropes = sb(sa, "ropes", [P, T])
    selg = sb(sa, "selg", [P, NG, P])
    msel = sb(sa, "msel", [AH, NG, P])
    onesel = sb(sa, "onesel", [1, P])
    ones = sb(sa, "ones", [1, T])
    lam = sb(sa, "lam", [P, 2])
    hT = sb(sa, "hT", [P, T])
    ctq = sb(sa, "ctq", [AQ, T])
    ctkv = sb(sa, "ctkv", [AQ, T])
    rot = sb(sa, "rot", [P, 3, T])
    qkT = sb(sa, "qkT", [P, 2, 2, T])
    hi = sb(sa, "hi", [P, T], F32R)
    q3 = sb(sa, "q3", [P, NG, T], F32R)
    k3 = sb(sa, "k3", [P, 2, NG, T], F32R)
    q3m = sb(sa, "q3m", [P, NG, T], F32R)
    vtok = sb(sa, "vtok", [P, 2, TT, AH, 32])
    mx = sb(sa, "mx", [P, TT, AH])
    nmT = sb(sa, "nmT", [AH, T])
    pT = sb(sa, "pT", [P, 2, TT, T])
    oG = sb(sa, "oG", [P, T])
    rden = sb(sa, "rden", [P, TT, AG])
    otok = sb(sa, "otok", [P, TT, AH, AD])
    oT = sb(sa, "oT", [P, T])
    yT = sb(sa, "yT", [P, T])

    loads = [(x0[:, :, :], a["x"].rearrange("b (t p) d -> p (b t) d", p=P)),
             (cT[:, :], a["cT"]), (wmod[:, :], a["wmod"]), (wdq[:, :], a["wdq"]), (wdkv[:, :], a["wdkv"]),
             (wq3[:, :, :], a["wq3"].rearrange("w k n -> k w n")), (wuk[:, :], a["wuk"]),
             (wk2[:, :, :], a["wk2"].rearrange("w k n -> k w n")), (wuv[:, :], a["wuv"]),
             (wo_a[:, :], a["wo_a"]), (bv[:, :], a["bv"].rearrange("(o n) -> o n", o=1).broadcast_to([P, D])),
             (ropec[:, :], a["ropec"]), (ropes[:, :], a["ropes"]),
             (selg[:, :, :], a["selg"]), (msel[:, :, :], a["msel"]), (onesel[:, :], a["onesel"]),
             (ones[:, :], a["ones"]), (lam[:, :], a["lam"])]
    for dst, src in loads:
        sp.dma(lambda e, d=dst, s=src: e.dma_start(d, s), s_a)
    loaded = (s_a, 16 * len(loads))

    eps_set = pool.do(lambda e: e.memset(epsc[:, :], EPS))
    m = pool.do(lambda e: e.memset(vtok[:, :, :, :, :], 0.0))
    v_ones = pool.do(lambda e: e.memset(vtok[:, :, :, :, AD:AD + 1], 1.0), m)
    ring = Banks([bank(4), bank(5)])

    m = act.do(lambda e: e.activation(sig[:, :], cT[:, :], ACT.Exp, scale=-1.0), loaded)
    m = dve.do(lambda e: e.tensor_scalar(sig[:, :], sig[:, :], 1.0, None, ALU.add), m, loaded)
    m = dve.do(lambda e: e.reciprocal(sig[:, :], sig[:, :]), m)
    m = dve.do(lambda e: e.tensor_tensor(sig[:, :], sig[:, :], cT[:, :], ALU.mult), m)
    i, bk, _ = ring.take()
    for j in range(6):
        mm = pe.do(lambda e, j=j, bk=bk: e.matmul(bk[:, j * B:(j + 1) * B], wmod[:, j * D:(j + 1) * D], sig[:, :],
                                                  start=True, stop=True), m, loaded, signal=j == 5)
    mod_v = mod[:, :, :].rearrange("p j b -> p (j b)")
    m = dve.do(lambda e, bk=bk: e.tensor_copy(mod_v, bk[:, 0:6 * B]), mm)
    ring.free[i] = m
    gate, sgn, mag = mod[:, 2::3, :], rot[:, 0, 0:2 * B], rot[:, 1, 0:2 * B]
    sgn, mag = (v.rearrange("p (j b) -> p j b", b=B) for v in (sgn, mag))
    m = dve.do(lambda e: e.tensor_scalar(mod[:, 1::3, :], mod[:, 1::3, :], 1.0, None, ALU.add), m)
    m = dve.do(lambda e: e.tensor_scalar(sgn, gate, 0.0, 2.0, ALU.is_ge, ALU.mult), m)
    m = dve.do(lambda e: e.scalar_tensor_tensor(out=mag, in0=gate, scalar=-1.0, in1=gate, op0=ALU.mult,
                                                op1=ALU.max), m)
    m = dve.do(lambda e: e.tensor_scalar(mag, mag, 0.25, None, ALU.max), m)
    m = dve.do(lambda e: e.scalar_tensor_tensor(out=gate, in0=sgn, scalar=-1.0, in1=mag, op0=ALU.add,
                                                op1=ALU.mult), m)
    mod_ready = m

    q_free = [None, None]
    state = {}

    def prepare(b):
        par = b % 2
        x_tile = lambda t: x0[:, b * TT + t, :]
        i, bk, free = ring.take()
        m = transpose_tiles(bk, x_tile, after=[loaded, free])
        ring.free[i] = act.do(lambda e, bk=bk: e.copy(xT[:, b, :], bk), m)
        m = normalise(x_tile, loaded)
        i, bk, free = ring.take()
        m = transpose_tiles(bk, lambda t: xn[:, t, :], after=[m, free])
        xn_free[0] = m
        h = act.do(lambda e, bk=bk: e.activation(hT[:, :], bk, ACT.Identity, bias=mod[:, 0, b:b + 1],
                                          scale=mod[:, 1, b:b + 1]), m, mod_ready, state.get("h_read"))
        ring.free[i] = h
        ct = []
        for w, dst, key in ((wdq, ctq, "b_dq"), (wdkv, ctkv, "b_dkv")):
            i, bk, free = ring.take()
            m = pe.do(lambda e, w=w, bk=bk: e.matmul(bk[0:AQ, :], w[:, :], hT[:, :], start=True, stop=True),
                      h, free)
            m = act.do(lambda e, bk=bk, dst=dst, key=key: e.activation(dst[:, :], bk[0:AQ, :], ACT.Identity,
                                                                       bias=vec(key, AQ)), m,
                       state.get("ct_read"))
            ring.free[i] = m
            ct.append(m)
        for n, (names, ws, srcs) in enumerate((
                (("bq_c", "bq_r", "bq_s"), (wq3[:, 0, :], wq3[:, 1, :], wq3[:, 2, :]), (ctq, ctq, ctq)),
                (("bk_c", "bk_r", "bk_s"), (wuk[:, :], wk2[:, 0, :], wk2[:, 1, :]), (ctkv, hT, hT)))):
            r = []
            for j in (1, 2, 0):
                i, bk, free = ring.take()
                m = pe.do(lambda e, bk=bk, w=ws[j], s=srcs[j]: e.matmul(bk, w, s[:, :], start=True, stop=True),
                          ct, free)
                if j:
                    tab = ropec if j == 1 else ropes
                    m = dve.do(lambda e, bk=bk, j=j, tab=tab, key=names[j]: e.scalar_tensor_tensor(
                        out=rot[:, j, :], in0=bk, scalar=vec(key), in1=tab[:, :], op0=ALU.add, op1=ALU.mult),
                        m, dve.last())
                else:
                    m = dve.do(lambda e, bk=bk, key=names[0]: e.scalar_tensor_tensor(
                        out=rot[:, 0, :], in0=bk, scalar=vec(key), in1=rot[:, 1, :], op0=ALU.add, op1=ALU.add),
                        m, r)
                ring.free[i] = m
                r.append(m)
            state["qk", par, n] = dve.do(lambda e, n=n: e.tensor_tensor(qkT[:, par, n, :], rot[:, 0, :],
                                                                        rot[:, 2, :], ALU.add), r, q_free[par])
        i, bk, free = ring.take()
        for t in range(TT):
            m = pe.do(lambda e, t=t, bk=bk: e.matmul(bk[:, t * P:(t + 1) * P], ctkv[:, t * P:(t + 1) * P],
                                                     wuv[:, :], start=True, stop=True), free, signal=t == TT - 1)
        state["ct_read"] = state["h_read"] = m
        bv_all = bv[:, :].rearrange("p (o h d) -> p o h d", o=1, h=AH).broadcast_to([P, TT, AH, AD])
        m = dve.do(lambda e, bk=bk: e.tensor_tensor(
            vtok[:, par, :, :, 0:AD], bk.rearrange("p (t h d) -> p t h d", t=TT, h=AH), bv_all, ALU.add),
            m, v_ones, state.get(("v_read", par)))
        ring.free[i] = state["v", par] = m
        for g in range(NG):
            pack(q3[:, g, :], par, 0, g, [], state.get("q3_read"))
            state["packed", par, g] = pack(k3[:, par, g, :], par, 1, g, [(onesel[:, :], ones[:, :])],
                                           state.get(("k3_read", par)))

    def pack(dst, par, n, g, extra, free_dst, *after):
        i, bk, free = ring.take()
        m = pe.do(lambda e: e.matmul(bk, selg[:, g, :], qkT[:, par, n, :], start=True, stop=not extra),
                  state["qk", par, n], free, signal=not extra)
        for lhsT, rhs in extra:
            m = pe.do(lambda e, lhsT=lhsT, rhs=rhs: e.matmul(bk, lhsT, rhs, start=False, stop=True), after)
        h = act.do(lambda e: e.copy(hi[:, :], bk), m, state.get("hi_read"))
        m = dve.do(lambda e: e.scalar_tensor_tensor(out=dst, in0=hi[:, :].bitcast(F32), scalar=lam[:, n:n + 1],
                                                    in1=bk, op0=ALU.mult, op1=ALU.add), h, free_dst)
        state["hi_read"] = m
        ring.free[i] = m
        return m

    def maxima(b, h):
        par, g, r = b % 2, h // AG, 32 * (h % AG)
        for t in range(TT):
            i, bk, free = ring.take()
            m = pe.do(lambda e, t=t, bk=bk: e.matmul(bk, q3[r:r + 32, g, t * P:(t + 1) * P], k3[r:r + 32, par, g, :],
                                                     start=True, stop=True), state["packed", par, g], free)
            ring.free[i] = dve.do(lambda e, t=t, bk=bk: e.tensor_reduce(mx[:, t, h:h + 1], bk, AX_X, ALU.max),
                                  m, state.get("mx_read"))
        if h == AH - 1:
            state["q3_read"] = m

    def spread_maxima(b):
        par = b % 2
        i, bk, free = ring.take()
        for t in range(TT):
            m = pe.do(lambda e, t=t: e.transpose(bk[0:AH, t * P:(t + 1) * P], mx[:, t, :], ident[:, :]),
                      dve.last(), free, signal=t == TT - 1)
        state["mx_read"] = m
        m = ring.free[i] = act.do(lambda e: e.mul(nmT[:, :], bk[0:AH, :], -1.0), m, state.get("nm_read"))
        for g in range(NG):
            state["packed_m", g] = pack(q3m[:, g, :], par, 0, g, [(msel[:, g, :], nmT[:, :])],
                                        state.get("q3m_read"), m)
        state["nm_read"] = pe.last()
        q_free[par] = pe.last()

    score_free = [None, None]
    pT_free = [None, None]
    exps = {}

    def exponentials(b, h):
        par, g, r = b % 2, h // AG, 32 * (h % AG)
        for half in range(2):
            for c in range(2 * half, 2 * half + 2):
                m = pe.do(lambda e, c=c: e.matmul(bank(c), k3[r:r + 32, par, g, c * P:(c + 1) * P],
                                                  q3m[r:r + 32, g, :], start=True, stop=True),
                          state["packed_m", g], score_free[half], signal=c % 2 == 1)
            m = act.do(lambda e, half=half: e.activation(pT[:, h % 2, 2 * half:2 * half + 2, :],
                                                         psum[:, 2 * half:2 * half + 2, :], ACT.Exp,
                                                         scale=1.0 / float(np.sqrt(np.float32(AH + AQ + AQ)))),
                       m, pT_free[h % 2])
            score_free[half] = m
        exps[h] = m
        if h == AH - 1:
            state["k3_read", par] = state["q3m_read"] = pe.last()

    out_free = [None, None]

    def weighted(b, h):
        par, g, hh = b % 2, h // AG, h % AG
        o = bank(6 + g % 2)
        for c in range(TT):
            m = pe.do(lambda e, c=c: e.matmul(o[32 * hh:32 * hh + 32, :], vtok[:, par, c, h, :], pT[:, h % 2, c, :],
                                              start=c == 0, stop=c == TT - 1, skip_group_check=True),
                      exps[h], state["v", par], out_free[g % 2] if hh == 0 else None, signal=c == TT - 1)
        pT_free[h % 2] = m
        if h == AH - 1:
            state["v_read", par] = m
        if hh == AG - 1:
            state["sums", g] = out_free[g % 2] = act.do(lambda e: e.copy(oG[:, :], o), m, state.get("oG_read"))

    def divide(b, g):
        i, bk, free = ring.take()
        m = transpose_tiles(bk, lambda t: oG[:, t * P:(t + 1) * P], after=[state["sums", g], free])
        state["oG_read"] = m
        o = bk.rearrange("p (t h c) -> p t h c", t=TT, h=AG)
        r = dve.do(lambda e: e.reciprocal(rden[:, :, :], o[:, :, :, AD]), m, state.get("rden_read"))
        den = rden[:, :, :].rearrange("p t (h o) -> p t h o", o=1).broadcast_to([P, TT, AG, AD])
        hs = slice(g * AG, g * AG + AG)
        m = dve.do(lambda e: e.tensor_tensor(otok[:, :, hs, :], o[:, :, :, 0:AD], den, ALU.mult), r,
                   state.get("otok_read"))
        ring.free[i] = state["otok"] = state["rden_read"] = m

    def finish_attention(b):
        i, bk, free = ring.take()
        m = transpose_tiles(bk, lambda t: otok[:, t, :, :].rearrange("p h d -> p (h d)"), after=[state["otok"], free])
        state["otok_read"] = m
        m = ring.free[i] = act.do(lambda e, bk=bk: e.copy(oT[:, :], bk), m)
        i, bk, free = ring.take()
        m = pe.do(lambda e, bk=bk: e.matmul(bk, wo_a[:, :], oT[:, :], start=True, stop=True), m, free)
        m = ring.free[i] = dve.do(lambda e, bk=bk: e.tensor_scalar(yT[:, :], bk, vec("b_o"), mod[:, 2, b:b + 1],
                                                                   ALU.add, ALU.mult), m)
        m = dve.do(lambda e: e.tensor_tensor(xT[:, b, :], xT[:, b, :], yT[:, :], ALU.add), m, act.last())
        i, bk, free = ring.take()
        m = transpose_tiles(bk, lambda t: xT[:, b, t * P:(t + 1) * P], after=[m, free])
        m = ring.free[i] = normalise(lambda t, bk=bk: bk[:, t * P:(t + 1) * P], m)
        i, bk, free = ring.take()
        m = transpose_tiles(bk, lambda t: xn[:, t, :], after=[m, free])
        xn_free[0] = m
        ring.free[i] = act.do(lambda e, bk=bk: e.activation(rT[:, b, :], bk, ACT.Identity, bias=mod[:, 3, b:b + 1],
                                                            scale=mod[:, 4, b:b + 1]), m)

    prepare(0)
    for h in range(AH):
        maxima(0, h)
    for b in range(B):
        spread_maxima(b)
        if b + 1 < B:
            prepare(b + 1)
        for h in range(AH):
            exponentials(b, h)
            if b + 1 < B:
                maxima(b + 1, h)
            if h:
                weighted(b, h - 1)
                if h % AG == 1 and h > AG:
                    divide(b, h // AG - 1)
        weighted(b, AH - 1)
        divide(b, NG - 1)
        finish_attention(b)
    sa.close()

    ends = start_stage("B")
    identb = sb(ctx, "identb", [P, P], BF16)
    masks = sb(ctx, "masks", [P, 2, 512], BF16)
    tabs = sb(ctx, "tabs", [P, 4, T])
    GT = 4
    pairsel = sb(ctx, "pairsel", [P, GT, 2 * GT])
    WCH = INNER // 2
    w_raw = sb(ctx, "w_raw", [P, 2, WCH])
    wqk_hi = sb(ctx, "wqk_hi", [P, 2, 2, WCH], F32R)
    wqk_lo = sb(ctx, "wqk_lo", [P, 2, 2, WCH], F32R)
    wv_hi = sb(ctx, "wv_hi", [P, 2, WCH], F32R)
    wv_lo = sb(ctx, "wv_lo", [P, 2, WCH], F32R)
    wo = sb(ctx, "wo", [P, HP, D])
    w1_hi = sb(ctx, "w1_hi", [P, 2 * DI], F32R)
    w1_lo = sb(ctx, "w1_lo", [P, 2 * DI], F32R)
    w2 = sb(ctx, "w2", [P, NC, D])
    xs = sb(ctx, "xs", [P, T])
    xs_hi = sb(ctx, "xs_hi", [P, 2, WIN + T], F32R)
    xs_lo = sb(ctx, "xs_lo", [P, 2, WIN + T], F32R)
    NRAW, NSWAP = 4, 4
    raw = sb(ctx, "raw", [P, NRAW, T])
    swapped = sb(ctx, "swapped", [P, NSWAP, T])
    sq = sb(ctx, "sq", [P, 2, T])
    u = sb(ctx, "u", [P, 2 * GT, T])
    nsq = sb(ctx, "nsq", [2 * GT, T])
    rn = sb(ctx, "rn", [P, 2, TT, 2 * GT])
    mhalf = sb(ctx, "mhalf", [P, TT * 2 * GT])
    rn2 = sb(ctx, "rn2", [P, TT, 4 * GT])
    rnT = sb(ctx, "rnT", [4 * GT, 2, T], F32R)
    selr = sb(ctx, "selr", [4 * GT, GT, P], F32R)
    qz = sb(ctx, "qz", [P, HP, NWIN, 2, WIN])
    kT = sb(ctx, "kT", [P, HP, WIN + T])
    HU = H // 2
    MU = HU // 2
    v1 = sb(ctx, "v1", [P, 2, HU, DH + 1])
    v0 = sb(ctx, "v0", [P, 2, HU, DH + 1])
    smax = sb(ctx, "smax", [P, HU])
    sdiff = sb(ctx, "sdiff", [P, HU, 2 * WIN])
    px = sb(ctx, "px", [P, HU, P])
    pxT = sb(ctx, "pxT", [P, HU, P])
    rd = sb(ctx, "rd", [P, HU])
    on = sb(ctx, "on", [P, HU, DH])
    onT = sb(ctx, "onT", [P, MU, P])
    hn_hi = sb(ctx, "hn_hi", [P, T], F32R)
    hn_lo = sb(ctx, "hn_lo", [P, T], F32R)
    gel = sb(ctx, "gel", [P, T])
    hid = sb(ctx, "hid", [P, NC, T])
    hn = hid[:, 0, :]

    cb = [(u[:, 1:3, :], a["masks"]), (tabs[:, :, :], a["tabs"]),
          (pairsel[:, :, :], a["pairsel"]), (u[0:4 * GT, 0, :], a["selr"].rearrange("k g p -> k (g p)"))]
    s_cb = sem("s_cb")
    sp.wait(ends)
    for dst, src in cb:
        sp.dma(lambda e, d=dst, s=src: e.dma_start(d, s), s_cb)
    constb = (s_cb, 16 * len(cb))

    landed = [0, 0]
    raw_free = [None, None]
    w_marks = {}

    def load_piece(src):
        half, n = state["half"], src.shape[1]
        state["half"] = 1 - half
        sp.dma(lambda e: e.dma_start(w_raw[:, half, 0:n], src), s_wraw[half], raw_free[half])
        landed[half] += 16
        return half, n, (s_wraw[half], landed[half])

    def split_piece(key, piece, hi_, lo_, free):
        half, n, ready = piece
        m = pool.do(lambda e: e.tensor_copy(hi_, w_raw[:, half, 0:n]), ready, free)
        m = pool.do(lambda e: e.tensor_tensor(lo_, w_raw[:, half, 0:n], hi_.bitcast(F32), ALU.subtract), m)
        w_marks[key] = raw_free[half] = m

    state["half"] = 0

    def weight_piece(i, kind, half):
        if kind == "v":
            dst = [w[:, half, :] for w in (wv_hi, wv_lo)]
            return (("v", half), a["wqkv"][i, :, 2 * INNER + half * WCH:2 * INNER + (half + 1) * WCH], *dst)
        if kind == "w1":
            c0, c1 = half * DI, (half + 1) * DI
            return (("w1", half), a["w1"][i, :, c0:c1], w1_hi[:, c0:c1], w1_lo[:, c0:c1])
        c0 = kind * INNER + half * WCH
        return ((kind, half), a["wqkv"][i, :, c0:c0 + WCH], wqk_hi[:, kind, half, :], wqk_lo[:, kind, half, :])

    def load_wo(i, half, *after):
        sp.dma(lambda e: e.dma_start(wo[:, half * HP // 2:(half + 1) * HP // 2, :],
                                     a["wo"][i, half * WCH:(half + 1) * WCH].rearrange("(m p) d -> p m d", p=P)),
               s_wo[half], after)

    def load_w2(i, *after):
        for c, (c0, n) in enumerate(DI_CHUNKS):
            sp.dma(lambda e, c=c, c0=c0, n=n: e.dma_start(w2[0:n, c, :], a["w2"][i, c0:c0 + n, :]), s_w2, after)

    load_wo(0, 0)
    load_wo(0, 1)
    load_w2(0)

    for t_ in (xs[:, 0:1], xs_hi[:, :, 0:WIN + 1], xs_lo[:, :, 0:WIN + 1], qz[:, :, :, :, :], kT[:, :, 0:WIN], px[:, :, :]):
        pool.do(lambda e, t_=t_: e.memset(t_.bitcast(F32) if t_.dtype == F32R else t_, 0.0))
    pool.do(lambda e: e.memset(mhalf[:, :], -0.5))
    s_v0, v0_in = [sem("s_v0_0"), sem("s_v0_1")], [0, 0]
    zeroed = pool.do(lambda e: e.memset(v1[:, :, :, DH:DH + 1], 1.0))
    selr_ready = pool.do(lambda e: e.tensor_copy(selr[:, :, :].rearrange("k g p -> k (g p)"), u[0:4 * GT, 0, :]), constb)
    pool.do(lambda e: e.tensor_copy(masks[:, :, :], u[:, 1:3, :]), constb)
    masks_ready = pool.do(lambda e: e.tensor_copy(identb[:, :], ident[:, :]), consts)

    def do_mm3(o, lhs, rhs, *after, signal=True):
        pe.do(lambda e: e.matmul(o, lhs[0], rhs[0], start=True, stop=False), *after, signal=False)
        pe.do(lambda e: e.matmul(o, lhs[0], rhs[1], start=False, stop=False), signal=False)
        return pe.do(lambda e: e.matmul(o, lhs[1], rhs[0], start=False, stop=True), signal=signal)

    st = {}

    halves = ((slice(0, 64), 0), (slice(64, P), 1))

    def shift(b):
        for rows, late in halves:
            m = act.do(lambda e, rows=rows, late=late: e.copy(xs[rows, late:], rT[rows, b, 0:T - late]), st.get(("res", b)),
                       st.get("xs_read"), zeroed)
        return m

    def shift_parts(b):
        free = st.get(("xsp_read", b % 2))
        for rows, late in halves:
            hi_, lo_ = (w[rows, b % 2, WIN + late:] for w in (xs_hi, xs_lo))
            r = rT[rows, b, 0:T - late]
            h_ = act.do(lambda e, hi_=hi_, r=r: e.copy(hi_, r), st.get(("res", b)), free, zeroed)
            m = dve.do(lambda e, hi_=hi_, lo_=lo_, r=r: e.tensor_tensor(lo_, r, hi_.bitcast(F32), ALU.subtract), h_,
                       st.get(("res", b)), free)
        st["rT_read", b] = m
        return m

    bank_free = [None] * 8
    s_swap = [sem(f"s_swap{k}") for k in range(NSWAP // 2)]
    swaps = [0] * (NSWAP // 2)
    u_free = [None] * (2 * GT)
    UT = 2 * MU

    LT = 2 * B * UT
    LB = 2 * B * TT

    def tile(n):
        i, n = divmod(n, LT)
        k, j = divmod(n, UT)
        return i, k // 2, k % 2, j // MU, (k % 2) * MU + j % MU

    NT = DEPTH * LT
    LAG = GT + 4

    def project():
        SUMS = 2
        NORM = 3
        marks = {}

        def heads(n):
            i, b, half, which, m_ = tile(n)
            x_ = (xs_hi[:, b % 2, WIN:], xs_lo[:, b % 2, WIN:])
            bk, slot, j, r_, s_ = n % 2, n % (2 * GT), n % 2, n % NRAW, n % NSWAP
            cols = slice((m_ % MU) * P, (m_ % MU + 1) * P)
            m = do_mm3(bank(bk), (wqk_hi[:, which, half, cols], wqk_lo[:, which, half, cols]), x_, marks["xs", b],
                       w_marks[which, half], bank_free[bk])
            st["wqk_read", which, half] = m
            c = marks["raw", n] = act.do(lambda e: e.mul(raw[:, r_, :], bank(bk), vec(("ks" if which else "qs", i))), m,
                                         st.get(("raw_read", r_)))
            bank_free[bk] = marks["sq", n] = act.do(lambda e: e.activation(sq[:, j, :], bank(bk), ACT.Square), m,
                                                    st.get(("sq_read", j)))
            a_ = dve.do(lambda e: e.tensor_tensor(u[:, slot, :], raw[:, r_, :], tabs[:, 2 * which, :], ALU.mult), c,
                        constb, u_free[slot])
            marks["cos", n] = st["raw_read", r_] = [a_]

        def swap(n):
            r_, s_ = n % NRAW, n % NSWAP
            for hp in range(2):
                for half in range(2):
                    f, t_ = 64 * hp + 32 * half, 64 * hp + 32 * (1 - half)
                    sp.dma(lambda e, f=f, t_=t_: e.dma_start(swapped[t_:t_ + 32, s_:s_ + 2, :],
                                                             raw[f:f + 32, r_:r_ + 2, :]),
                           s_swap[s_ // 2], marks["raw", n], marks["raw", n + 1], st.get(("swapped_read", s_)),
                           st.get(("swapped_read", s_ + 1)))
            swaps[s_ // 2] += 64
            for k in range(2):
                marks["swap", n + k] = (s_swap[s_ // 2], swaps[s_ // 2])
                st["raw_read", r_ + k] = [marks["swap", n + k]] + st["raw_read", r_ + k]

        def rotate(n):
            which = tile(n)[3]
            slot, s_ = n % (2 * GT), n % NSWAP
            m = pool.do(lambda e: e.tensor_tensor(swapped[:, s_, :], swapped[:, s_, :], tabs[:, 2 * which + 1, :],
                                                 ALU.mult), marks["swap", n])
            marks["u", n] = st["swapped_read", s_] = pool.do(lambda e: e.tensor_tensor(
                u[:, slot, :], u[:, slot, :], swapped[:, s_, :], ALU.add), m, marks["cos", n])

        def square_sums(n):
            bk, k = SUMS, n % GT
            m = pe.do(lambda e: e.matmul(bank(bk)[0:2 * GT, :], pairsel[:, k, :], sq[:, n % 2, :], start=k == 0,
                                         stop=k == GT - 1), marks["sq", n], constb, bank_free[bk])
            st["sq_read", n % 2] = m
            if k == GT - 1:
                bank_free[bk] = marks["rows", n // GT] = act.do(lambda e: e.copy(nsq[:, :], bank(bk)[0:2 * GT, :]), m,
                                                st.get("nsq_read"))

        def norms(g):
            bk = NORM
            src = bank(bk)[:, 0:TT * 2 * GT]
            for t in range(TT):
                m = pe.do(lambda e, t=t: e.transpose(src[:, t * 2 * GT:(t + 1) * 2 * GT], nsq[:, t * P:(t + 1) * P],
                                                     ident[0:2 * GT, 0:2 * GT]), marks["rows", g], bank_free[bk], signal=t == TT - 1)
            st["nsq_read"] = m
            r3 = rn[:, g % 2, :, :]
            r = r3.rearrange("p t h -> p (t h)")
            m = bank_free[bk] = dve.do(lambda e: e.tensor_scalar(r, src, 1e-24, None, ALU.max), m,
                                       st.get(("rn_read", g % 2)))
            marks["norm", g] = pool.do(lambda e: e.tensor_tensor(r, r, mhalf[:, :], ALU.pow), m)

        def norm_parts(g):
            r3, r_hi, r_lo = rn[:, g % 2, :, :], rn2[:, :, 0:2 * GT], rn2[:, :, 2 * GT:]
            m = dve.do(lambda e: e.tensor_copy(r_hi.bitcast(F32R), r3), marks["norm", g], st.get("rn2_read"))
            m = dve.do(lambda e: e.tensor_tensor(r_lo, r3, r_hi, ALU.subtract), m)
            st["rn_read", g % 2] = marks["parts", g] = m

        def norm_rows(g):
            bk = NORM
            for t in range(TT):
                m = pe.do(lambda e, t=t: e.transpose(bank(bk)[0:4 * GT, t * P:(t + 1) * P], rn2[:, t, :], ident[:, :]),
                          marks["parts", g], bank_free[bk], signal=t == TT - 1)
            st["rn2_read"] = m
            marks["rn", g] = bank_free[bk] = act.do(lambda e: e.copy(rnT[:, g % 2, :], bank(bk)[0:4 * GT, :]), m,
                                                    st.get(("rnT_read", g % 2)))

        def scale(n):
            _, _, half, which, m_ = tile(n)
            g, k, slot = n // GT, n % GT, n % (2 * GT)
            bk = NORM
            m = pe.do(lambda e: e.matmul(bank(bk), selr[:, k, :], rnT[:, g % 2, :], start=True, stop=True),
                      marks["rn", g], bank_free[bk], selr_ready)
            st["rnT_read", g % 2] = m
            if which == 0:
                for hp in range(2):
                    s_ = slice(64 * hp, 64 * hp + 64)
                    m2 = dve.do(lambda e, s_=s_, hp=hp: e.tensor_tensor(
                        qz[s_, m_, :, hp, :], u[s_, slot, :].rearrange("p (w q) -> p w q", q=WIN),
                        bank(bk)[s_, :].rearrange("p (w q) -> p w q", q=WIN), ALU.mult), m, marks["u", n], zeroed,
                                st.get(("qk_read", half)))
            else:
                m2 = dve.do(lambda e: e.tensor_tensor(kT[:, m_, WIN:], u[:, slot, :], bank(bk), ALU.mult), m,
                            marks["u", n], zeroed, st.get(("qk_read", half)))
            bank_free[bk] = u_free[slot] = st["scaled", which, m_] = m2

        marks["xs", 0] = shift_parts(0)
        for n in range(NT + LAG):
            if n >= LAG:
                scale(n - LAG)
            if n % GT == 3 and GT < n <= NT + 3:
                norm_parts(n // GT - 1)
            if (n + 1) % (2 * UT) == 0 and n + 1 < NT:
                following = tile(n + 1)[1]
                marks["xs", following] = shift_parts(following)
            if n < NT:
                heads(n)
            if 1 <= n <= NT:
                square_sums(n - 1)
            if n % 2 == 0 and 4 <= n < NT + 4:
                rotate(n - 4)
                rotate(n - 3)
            if n % 2 == 1 and n < NT:
                swap(n - 1)
            if n % GT == 1 and GT < n <= NT + 1:
                norms(n // GT - 1)
            if n % GT == 3 and GT < n <= NT + 3:
                norm_rows(n // GT - 1)
            yield n

    ring = [0]

    def take():
        ring[0] += 1
        return 5 + ring[0] % 3

    def attention(pieces):
        mk = {}

        def where(n):
            i, n = divmod(n, LB)
            k, t = divmod(n, TT)
            return i, k // 2, k % 2, t

        def scores(n):
            _, _, half, t = where(n)
            first = 1 if t == 0 else 0
            pe.do(lambda e: e.matmul(bank(4), identb[:, :], masks[:, first, :], start=True, stop=False,
                                     skip_group_check=True), bank_free[4], masks_ready, signal=False)
            for j in range(MU):
                m_ = half * MU + j
                for s_ in range(2):
                    for w_ in range(2):
                        win = 4 * t + 2 * w_ + s_
                        o = bank(4)[64 * w_:64 * w_ + 64, (j * 2 + s_) * 64:][:, 0:64]
                        last = j == MU - 1 and s_ == 1 and w_ == 1
                        m = pe.do(lambda e, o=o, m_=m_, win=win, last=last: e.matmul(
                            o, qz[:, m_, win, :, :].rearrange("p h q -> p (h q)"), kT[:, m_, win * WIN:(win + 2) * WIN],
                            start=False, stop=last, skip_group_check=True),
                                  st["scaled", 0, m_], st["scaled", 1, m_], signal=last)
            if t == TT - 1:
                st["qk_read", half] = m
            sv = bank(4).rearrange("p (k j) -> p k j", j=2 * WIN)
            m = dve.do(lambda e: e.tensor_reduce(smax[:, :], sv, AX_X, ALU.max), m)
            mb = smax[:, :].rearrange("p (k o) -> p k o", o=1).broadcast_to([P, HU, 2 * WIN])
            m = dve.do(lambda e: e.tensor_tensor(sdiff[:, :, :], sv, mb, ALU.subtract), m, st.get("sdiff_read"))
            bank_free[4] = m
            for w_ in range(2):
                r = slice(64 * w_, 64 * w_ + 64)
                m2 = act.do(lambda e, r=r: e.activation(px[r, :, r], sdiff[r, :, :], ACT.Exp, scale=8.0), m,
                            st.get("px_read"), zeroed)
            st["sdiff_read"] = mk["px", n] = m2

        def values(n):
            i, b, half, t = where(n)
            par = n % 2
            now, before = v1[:, par, :, :], v1[:, 1 - par, :, :]
            bk = take()
            x_ = [p_[:, b % 2, WIN + t * P:WIN + (t + 1) * P] for p_ in (xs_hi, xs_lo)]
            m = do_mm3(bank(bk), x_, [w_[:, half, :] for w_ in (wv_hi, wv_lo)], w_marks["v", half],
                       bank_free[bk])
            st["wv_read", half] = m
            bank_free[bk] = c = mk["v1", n] = act.do(lambda e: e.copy(
                now[:, :, 0:DH], bank(bk).rearrange("p (h d) -> p h d", d=DH)), m, zeroed, mk.get(("products", n - 2)),
                                                     mk.get(("v0", n - 1)))
            st["xsp_read", b % 2] = m
            free = mk.get(("products", n - 2))
            if t == 0:
                z = pool.do(lambda e: e.memset(v0[0:WIN, par, :, :], 0.0), free)
            else:
                z = None
                sp.dma(lambda e: e.dma_start(v0[0:WIN, par, :, :], before[P - WIN:P, :, :]), s_v0[par], mk["v1", n - 1],
                       free)
                v0_in[par] += 16
            sp.dma(lambda e: e.dma_start(v0[WIN:P, par, :, :], now[0:P - WIN, :, :]), s_v0[par], c, free)
            v0_in[par] += 16
            mk["v0", n] = [z, (s_v0[par], v0_in[par])]

        def transposes(n):
            for q in range(2):
                bk = take()
                for k in range(4):
                    m = pe.do(lambda e, k=k, q=q, bk=bk: e.transpose(bank(bk)[:, k * P:(k + 1) * P], px[:, 4 * q + k, :],
                                                                     ident[:, :]), mk["px", n], bank_free[bk],
                              signal=k == 3)
                eng = act if q == 0 else dve
                for hp in range(2):
                    dst = pxT[:, 4 * q:4 * q + 4, hp * 64:hp * 64 + 64].rearrange("p k (w q) -> p k w q", w=2)
                    src = bank(bk).rearrange("p (k w h q) -> p k w h q", w=2, h=2, q=WIN)[:, :, :, hp, :]
                    f = (lambda e, dst=dst, src=src: e.copy(dst, src)) if eng is act else \
                        (lambda e, dst=dst, src=src: e.tensor_copy(dst, src))
                    m2 = eng.do(f, m, mk.get(("products", n - 1)))
                mk["pxT", n, q] = bank_free[bk] = m2
            st["px_read"] = m

        def apply(n, g):
            bk = take()
            hs = slice(4 * g, 4 * g + 4)
            for h in range(4):
                j, hp = divmod(4 * g + h, 2)
                for s_ in range(2):
                    lhs = pxT[:, 2 * j + s_, hp * 64:hp * 64 + 64]
                    rhs = (v1 if s_ else v0)[:, n % 2, 4 * g + h, :]
                    o = bank(bk)[64 * s_:64 * s_ + 64, h * (DH + 1):(h + 1) * (DH + 1)]
                    m = pe.do(lambda e, o=o, lhs=lhs, rhs=rhs: e.matmul(o, lhs, rhs, start=True, stop=True),
                              mk["pxT", n, g], mk["v1", n], mk["v0", n], bank_free[bk], signal=h == 3 and s_ == 1)
            ov = bank(bk)[:, 0:4 * (DH + 1)].rearrange("p (h d) -> p h d", d=DH + 1)
            r = dve.do(lambda e: e.reciprocal(rd[:, hs], ov[:, :, DH]), m)
            den = rd[:, hs].rearrange("p (h o) -> p h o", o=1).broadcast_to([P, 4, DH])
            bank_free[bk] = mk["on", n, g] = dve.do(lambda e: e.tensor_tensor(on[:, hs, :], ov[:, :, 0:DH], den,
                                                                              ALU.mult), r, st.get("on_read"))
            if g:
                mk["products", n] = m

        def output(n):
            bk = take()
            for k in range(MU):
                m = pe.do(lambda e, k=k: e.transpose(
                    bank(bk)[:, k * P:(k + 1) * P], on[:, 2 * k:2 * k + 2, :].rearrange("p h d -> p (h d)"), ident[:, :]),
                          mk["on", n, 0], mk["on", n, 1], bank_free[bk], signal=k == MU - 1)
            bank_free[bk] = mk["onT", n] = act.do(lambda e: e.copy(onT[:, :, :].rearrange("p k c -> p (k c)"), bank(bk)),
                                                  m, st.get("onT_read"))
            st["on_read"] = m

        def product(n):
            i, b, half, t = where(n)
            bk = take()
            y = bank(bk)[:, 0:P]
            for j in range(MU):
                m = pe.do(lambda e, j=j: e.matmul(y, wo[:, half * MU + j, :], onT[:, j, :], start=j == 0, stop=j == MU - 1),
                          mk["onT", n], bank_free[bk], (s_wo[half], 16 * (i + 1)), signal=j == MU - 1)
            st["onT_read"] = st["wo_read", half] = m
            y_ = y.rearrange("p (s w q) -> p w s q", w=2, s=2)
            r = rT[:, b, t * P:(t + 1) * P].rearrange("p (w s q) -> p w s q", w=2, s=2)
            bank_free[bk] = st["res", b] = dve.do(lambda e: e.tensor_tensor(r, y_, r, ALU.add), m, dve.last())

        values(0)
        scores(0)
        N = DEPTH * LB
        for n in range(N):
            transposes(n)
            if n:
                output(n - 1)
            yield
            if n + 1 < N:
                scores(n + 1)
            if n:
                product(n - 1)
            apply(n, 0)
            yield
            if n + 1 < N:
                values(n + 1)
            apply(n, 1)
            pieces(n)
        output(N - 1)
        product(N - 1)

    ff = {}

    def feed_forward(i, b):
        def token_major():
            m = shift(b)
            bk = take()
            m = transpose_tiles(bank(bk), lambda t: xs[:, t * P:(t + 1) * P], after=[m, bank_free[bk]])
            st["xs_read"] = m
            bank_free[bk] = ff["x"] = act.do(lambda e: e.copy(xn[:, :, :].rearrange("p t d -> p (t d)"), bank(bk)), m,
                                             xn_free[0])

        def statistics():
            for t in range(TT):
                m = dve.do(lambda e, t=t: e.bn_stats(stats[:, t, :], xn[:, t, :]), ff["x"], dve.last())
            for t in range(TT):
                m2 = dve.do(lambda e, t=t: e.bn_aggr(mv[:, t, :], stats[:, t, :]), m)
            m = pool.do(lambda e: e.tensor_scalar(rstd[:, :], mv[:, :, 1], EPS, None, ALU.add), m2)
            ff["rstd"] = pool.do(lambda e: e.tensor_tensor(rstd[:, :], rstd[:, :], mhalf[:, 0:TT], ALU.pow), m)

        def feature_major():
            for t in range(TT):
                m = dve.do(lambda e, t=t: e.tensor_scalar(xn[:, t, :], xn[:, t, :], mv[:, t, 0:1], rstd[:, t:t + 1],
                                                          ALU.subtract, ALU.mult), ff["rstd"])
            bk = take()
            m = transpose_tiles(bank(bk), lambda t: xn[:, t, :], after=[m, bank_free[bk]])
            xn_free[0] = m
            m = act.do(lambda e: e.activation(hn, bank(bk), ACT.Identity, bias=vec(("b", i)), scale=vec(("g", i))),
                       m, st.get("hid_read"))
            bank_free[bk] = m
            h_ = act.do(lambda e: e.copy(hn_hi[:, :], hn), m, st.get("hns_read"))
            ff["h"] = dve.do(lambda e: e.tensor_tensor(hn_lo[:, :], hn, hn_hi[:, :].bitcast(F32), ALU.subtract), h_,
                             st.get("hns_read"))

        def up(c):
            c0, n = DI_CHUNKS[c]
            x_ = (hn_hi[:, :], hn_lo[:, :])
            kg, ka = take(), take()
            pa, pg = bank(ka)[0:n, :], bank(kg)[0:n, :]
            mg = do_mm3(pg, (w1_hi[:, DI + c0:DI + c0 + n], w1_lo[:, DI + c0:DI + c0 + n]), x_, ff["h"],
                        bank_free[kg], w_marks["w1", 0], w_marks["w1", 1])
            ma = do_mm3(pa, (w1_hi[:, c0:c0 + n], w1_lo[:, c0:c0 + n]), x_, bank_free[ka])
            g_ = act.do(lambda e: e.activation(gel[0:n, :], pg, ACT.Gelu, bias=vec(("b1g", i, c), n)), mg,
                        st.get("gel_read"))
            bank_free[kg] = g_
            bank_free[ka] = st["gel_read"] = ff["hid"] = dve.do(lambda e: e.scalar_tensor_tensor(
                out=hid[0:n, c, :], in0=pa, scalar=vec(("b1a", i, c), n), in1=gel[0:n, :], op0=ALU.add,
                op1=ALU.mult), ma, g_, ff["h"], st.get("hid_read"))
            st["hns_read"] = st["w1_read"] = ma

        def down():
            bk = take()
            for c, (c0, n) in enumerate(DI_CHUNKS):
                m = pe.do(lambda e, c=c, n=n: e.matmul(bank(bk), w2[0:n, c, :], hid[0:n, c, :], start=c == 0,
                                                       stop=c == NC - 1), ff["hid"], bank_free[bk],
                          (s_w2, 16 * NC * (i + 1)), signal=c == NC - 1)
            st["hid_read"] = st["w2_read"] = m
            bank_free[bk] = st["res", b] = dve.do(lambda e: e.scalar_tensor_tensor(
                out=rT[:, b, :], in0=bank(bk), scalar=vec(("b2", i)), in1=rT[:, b, :], op0=ALU.add, op1=ALU.add), m)

        return [token_major, statistics, feature_major] + [lambda c=c: up(c) for c in range(NC)] + [down]

    def write_out(b):
        m = dve.do(lambda e: e.scalar_tensor_tensor(out=xT[:, b, :], in0=rT[:, b, :], scalar=mod[:, 5, b:b + 1],
                                                    in1=xT[:, b, :], op0=ALU.mult, op1=ALU.add), st["res", b])
        bk = take()
        m = transpose_tiles(bank(bk), lambda t: xT[:, b, t * P:(t + 1) * P], after=[m, bank_free[bk]])
        bank_free[bk] = m = act.do(lambda e: e.copy(xn[:, :, :].rearrange("p t d -> p (t d)"), bank(bk)), m, xn_free[0])
        sp.dma(lambda e: e.dma_start(out[b].rearrange("(t p) d -> p t d", p=P), xn[:, :, :]), s_out, m)
        xn_free[0] = (s_out, 16 * (b + 1))

    BATCH = 2 * TT
    blocks = {}
    staged = {}

    def at(n, fn):
        blocks.setdefault(n, []).append(fn)

    def stage_weights(n, i, kind, half, key, load_at=None):
        k_, src, hi_, lo_ = weight_piece(i, kind, half)

        def load():
            staged[k_] = load_piece(src)
        at(n, load)
        at(n + 1, lambda: split_piece(k_, staged[k_], hi_, lo_, st.get(key)))

    for i in range(DEPTH):
        for b in range(B):
            n = i * LB + (b + 1) * BATCH
            pieces = feed_forward(i, b)
            for k, piece in enumerate(pieces):
                at(n + 1 + k, piece)
            if i == DEPTH - 1:
                at(n + 1 + len(pieces), lambda b=b: write_out(b))
        if i + 1 == DEPTH:
            break
        n = (i + 1) * LB
        for half in range(2):
            stage_weights(n - 2 - (1 - half) * (TT - 1), i + 1, "v", half, ("wv_read", half))
            at(n + 1 - (1 - half) * TT, lambda i=i, half=half: load_wo(i + 1, half, st["wo_read", half]))
            for which in range(2):
                stage_weights(n - UT - (1 - half) * UT // 2 + which, i + 1, which, half, ("wqk_read", which, half))
            stage_weights(n + 1 + 3 + NC + half, i + 1, "w1", half, "w1_read")
        at(n + 2 + 3 + NC, lambda i=i: load_w2(i + 1, st["w2_read"]))

    for which, half in ((0, 0), (1, 0), (0, 1), (1, 1), ("v", 0), ("v", 1), ("w1", 0), ("w1", 1)):
        key, src, hi_, lo_ = weight_piece(0, which, half)
        split_piece(key, load_piece(src), hi_, lo_, None)

    def pieces(n):
        for fn in blocks.pop(n, []):
            fn()

    steps = project()
    for _ in range(2 * UT + 1):
        next(steps)
    for _ in attention(pieces):
        next(steps, None)
    for n in sorted(blocks):
        pieces(n)
    sp.wait((s_out, 16 * B))

    block = ctx.enter_context(nc.Block())

    def run(steps):
        def body(e):
            for step in steps:
                step(e)
        return body

    block.tensor(run(pe.steps))
    block.vector(run(dve.steps))
    block.scalar(run(act.steps))
    block.gpsimd(run(pool.steps))
    block.sync(run(sp.steps))
    ctx.close()


def constants():
    f = np.float32
    c = {"ident": np.eye(P, dtype=f)}
    pos = np.arange(T, dtype=f)[:, None]
    ids = np.arange(D // 2, dtype=f)
    theta = (f(10000.0) ** (f(-2.0) * ids) / f(D // 2)).astype(f)
    r = (pos * theta[None, :]).astype(f)
    c["ropec"] = np.ascontiguousarray(np.repeat(np.cos(r), 2, axis=1).T)
    sgn = np.where(np.arange(D) % 2 == 0, -1, 1).astype(f)
    c["ropes"] = np.ascontiguousarray(np.repeat(np.sin(r), 2, axis=1).T * sgn[:, None])
    selg, msel, onesel = np.zeros((P, NG, P), f), np.zeros((AH, NG, P), f), np.zeros((1, P), f)
    lam = np.zeros((P, 2), f)
    for g in range(NG):
        for h in range(AG):
            for k in range(3):
                for d in range(AD):
                    selg[(AG * g + h) * AD + d, g, 32 * h + AD * k + d] = 1
            msel[AG * g + h, g, 32 * h + 3 * AD] = 1
    for h in range(AG):
        onesel[0, 32 * h + 3 * AD] = 1
        lam[32 * h + 2 * AD:32 * h + 3 * AD, 0] = -1
        lam[32 * h + AD:32 * h + 2 * AD, 1] = -1
    c.update(selg=selg, msel=msel, onesel=onesel, lam=lam, ones=np.ones((1, T), f))
    half = np.arange(0, DH, 2, dtype=f)
    inv_freq = (f(1.0) / f(10000.0) ** (half / f(DH))).astype(f)
    t = np.arange(T, dtype=f)
    fr = (t[:, None] * inv_freq[None, :]).astype(f)
    fr = np.concatenate([fr, fr], -1)
    base = ((half + f(0.4 * DH)) / f(1.4 * DH)).astype(f)
    power = ((t - T // 2) / f(WIN // 2)).astype(f)
    sc = (base[None, :] ** power[:, None]).astype(f)
    sc = np.concatenate([sc, sc], -1)
    inv = (f(1.0) / sc).astype(f)
    s2 = np.where(np.arange(DH) < DH // 2, -1, 1).astype(f)
    two = lambda z: np.tile(z.astype(f).T, (2, 1))
    c["tabs"] = np.ascontiguousarray(np.stack([two(np.cos(fr) * sc), two(np.sin(fr) * sc * s2),
                                               two(np.cos(fr) * inv), two(np.sin(fr) * inv * s2)], axis=1))
    pairsel = np.zeros((P, 4, 8), f)
    for k in range(4):
        pairsel[0:64, k, 2 * k] = 1
        pairsel[64:, k, 2 * k + 1] = 1
    c["pairsel"] = pairsel
    selr = np.zeros((16, 4, P), f)
    for k in range(4):
        for hp in range(2):
            for part in range(2):
                selr[8 * part + 2 * k + hp, k, 64 * hp:64 * hp + 64] = 1
    c["selr"] = selr
    q, j = np.arange(WIN)[:, None], np.arange(2 * WIN)[None, :]
    ok = (j >= q) & (j <= q + WIN)
    masks = np.zeros((P, 2, 4, 2, 2 * WIN), f)
    masks[:] = np.where(np.tile(ok, (4, 1)), 0.0, NEG)[:, None, None, None, :]
    masks[0:64, 1, :, 0, 0:WIN] = NEG
    c["masks"] = masks.reshape(P, 2, 512)
    return c


def kernel(**inputs):
    import concourse.bacc as bacc
    from concourse.bass_utils import run_bass_kernel_spmd

    x = {k.replace("L0_", ""): np.ascontiguousarray(v) for k, v in inputs.items()}
    pair = np.arange(D).reshape(-1, 2)[:, ::-1].reshape(-1)
    half = np.arange(DH).reshape(2, -1)[::-1].reshape(-1)
    arrays = constants()
    vecs = np.zeros((P, NVEC), np.float32)

    def put(key, v):
        vecs[0:len(v), VEC[key]] = v

    put("bq_c", x["attn_Wu_q_b"])
    put("bq_r", x["attn_Wq_r_b"])
    put("bq_s", x["attn_Wq_r_b"][pair])
    put("bk_c", x["attn_Wu_k_b"])
    put("bk_r", x["attn_Wk_r_b"])
    put("bk_s", x["attn_Wk_r_b"][pair])
    put("b_o", x["attn_Wo_b"])
    put("b_dq", x["attn_Wd_q_b"])
    put("b_dkv", x["attn_Wd_kv_b"])
    for i in range(DEPTH):
        for key, v in (("qs", x["ffn_q_scale"][i]), ("ks", x["ffn_k_scale"][i])):
            put((key, i), np.concatenate([v, v]))
        put(("g", i), x["ffn_ln_g"][i])
        put(("b", i), x["ffn_ln_b"][i])
        put(("b2", i), x["ffn_b2"][i])
        for c, (c0, n) in enumerate(DI_CHUNKS):
            put(("b1a", i, c), x["ffn_b1"][i, c0:c0 + n])
            put(("b1g", i, c), x["ffn_b1"][i, DI + c0:DI + c0 + n])
    arrays.update(
        vecs=vecs, x=x["attn_x"], cT=np.ascontiguousarray(x["c"].T), wmod=x["wmod"], wdq=x["attn_Wd_q_w"],
        wdkv=x["attn_Wd_kv_w"],
        wq3=np.stack([x["attn_Wu_q_w"], x["attn_Wq_r_w"], x["attn_Wq_r_w"][:, pair]]),
        wuk=x["attn_Wu_k_w"], wk2=np.stack([x["attn_Wk_r_w"], x["attn_Wk_r_w"][:, pair]]),
        wuv=x["attn_Wu_v_w"], wo_a=x["attn_Wo_w"], bv=x["attn_Wu_v_b"],
        wqkv=x["ffn_Wqkv"], wo=x["ffn_Wo"], w1=x["ffn_W1"],
        w2=x["ffn_W2"])
    nc = bacc.Bacc("TRN2", target_bir_lowering=False, num_devices=1)
    aps = {n: nc.dram_tensor(f"in_{n}", v.shape, mybir.dt.from_np(v.dtype), kind="ExternalInput").ap()
           for n, v in arrays.items()}
    out = nc.dram_tensor("out_x", (B, T, D), F32, kind="ExternalOutput").ap()
    build(nc, aps, out)
    r = run_bass_kernel_spmd(nc, [{f"in_{n}": v for n, v in arrays.items()}], core_ids=[0])
    return r.results[0]["out_x"]
```

```python
from contextlib import ExitStack

import numpy as np
import concourse.bass as bass
from concourse import mybir

F32 = mybir.dt.float32
F32R = mybir.dt.float32r
BF16 = mybir.dt.bfloat16
ALU = mybir.AluOpType
ACT = mybir.ActivationFunctionType
AX_X = mybir.AxisListType.X

P = 128
B, T, D = 4, 512, 128
TT = T // P
AH, AD = 16, 8
AQ = 64
AG = 4
NG = AH // AG
DEPTH, H, DH, WIN = 6, 16, 64, 32
INNER = H * DH
HP = H // 2
NWIN = T // WIN
DI = int(D * 4 * 2 / 3)
DI_CHUNKS = [(c, min(P, DI - c)) for c in range(0, DI, P)]
NC = len(DI_CHUNKS)
EPS = 1e-5
NEG = -1e30


VEC = {}
for _n in ("bq_c", "bq_r", "bq_s", "bk_c", "bk_r", "bk_s", "b_o", "b_dq", "b_dkv"):
    VEC[_n] = len(VEC)
for _i in range(DEPTH):
    for _n in ("qs", "ks", "g", "b", "b2"):
        VEC[_n, _i] = len(VEC)
    for _c in range(NC):
        VEC["b1a", _i, _c] = len(VEC)
        VEC["b1g", _i, _c] = len(VEC)
NVEC = len(VEC)


class Engine:

    def __init__(self):
        self.steps, self.sem, self.count, self.waited = [], None, 0, {}

    def start_stage(self, sem):
        self.sem, self.count = sem, 0

    def wait(self, *marks):
        for m in marks:
            if isinstance(m, (list, tuple)) and m and isinstance(m[0], (list, tuple, type(None))):
                self.wait(*m)
            elif m:
                sem, value = m
                if self.waited.get(sem.name, 0) < value:
                    self.waited[sem.name] = value
                    self.steps.append(lambda e, s=sem, v=value: e.wait_ge(s, v))

    def do(self, fn, *after, signal=True):
        self.wait(*after)
        if not signal:
            self.steps.append(fn)
            return None
        self.count += 1
        sem = self.sem
        self.steps.append(lambda e: fn(e).then_inc(sem, 1))
        return (sem, self.count)

    def dma(self, fn, sem, *after):
        self.wait(*after)
        self.steps.append(lambda e: fn(e).then_inc(sem, 16))

    def last(self):
        return (self.sem, self.count) if self.count else None


class Banks:

    def __init__(self, banks):
        self.banks, self.free, self.at = banks, [None] * len(banks), 0

    def take(self):
        i = self.at % len(self.banks)
        self.at += 1
        return i, self.banks[i], self.free[i]


def build(nc, a, out):
    ctx = ExitStack()
    sem = lambda name: ctx.enter_context(nc.semaphore(name))

    def sb(scope, name, shape, dt=F32):
        return scope.enter_context(nc.sbuf_tensor(name, shape, dt))

    pe, dve, act, pool, sp = (Engine() for _ in range(5))
    engines = {"pe": pe, "dve": dve, "act": act, "pool": pool}

    def start_stage(n):
        ends = [e.last() for e in engines.values()]
        for name, e in engines.items():
            e.start_stage(sem(f"s_{name}_{n}"))
        for e in engines.values():
            e.wait(ends)
        return ends

    psum = ctx.enter_context(nc.psum_tensor("psum", [P, 8, 512], F32))
    bank = lambda i: psum[:, i, :]

    ident = sb(ctx, "ident", [P, P])
    vecs = sb(ctx, "vecs", [P, NVEC])
    xT = sb(ctx, "xT", [P, B, T])
    rT = sb(ctx, "rT", [P, B, T])
    mod = sb(ctx, "mod", [P, 6, B])
    stats = sb(ctx, "stats", [P, TT, 6])
    mv = sb(ctx, "mv", [P, TT, 2])
    rstd = sb(ctx, "rstd", [P, TT])
    epsc = sb(ctx, "epsc", [P, 1])
    xn = sb(ctx, "xn", [P, TT, P])

    s_const, s_x, s_a, s_out = sem("s_const"), sem("s_x"), sem("s_a"), sem("s_out")
    s_wraw = [sem("s_wraw0"), sem("s_wraw1")]
    s_wo = [sem("s_wo0"), sem("s_wo1")]
    s_w2 = sem("s_w2")
    vec = lambda key, n=P: vecs[0:n, VEC[key]:VEC[key] + 1]

    sp.dma(lambda e: e.dma_start(ident[:, :], a["ident"]), s_const)
    sp.dma(lambda e: e.dma_start(vecs[:, :], a["vecs"]), s_const)
    consts = (s_const, 32)

    def transpose_tiles(bank_out, src, n_part=P, after=()):
        for t in range(TT):
            m = pe.do(lambda e, t=t: e.transpose(bank_out[:, t * P:(t + 1) * P], src(t), ident[:, :]),
                      after, consts, signal=t == TT - 1)
        return m

    xn_free = [None]

    def normalise(src, ready):
        for t in range(TT):
            m = dve.do(lambda e, t=t: e.bn_stats(stats[:, t, :], src(t)), ready, dve.last())
        for t in range(TT):
            m2 = dve.do(lambda e, t=t: e.bn_aggr(mv[:, t, :], stats[:, t, :]), m)
        m = act.do(lambda e: e.activation(rstd[:, :], mv[:, :, 1], ACT.Sqrt, bias=epsc[:, 0:1]), m2, eps_set)
        m = dve.do(lambda e: e.reciprocal(rstd[:, :], rstd[:, :]), m)
        for t in range(TT):
            r = dve.do(lambda e, t=t: e.tensor_scalar(xn[:, t, :], src(t), mv[:, t, 0:1], rstd[:, t:t + 1],
                                                      ALU.subtract, ALU.mult), m, xn_free[0])
        return r

    for n, e in engines.items():
        e.start_stage(sem(f"s_{n}_A"))
    sa = ExitStack()
    x0 = sb(sa, "x0", [P, B * TT, P])
    cT = sb(sa, "cT", [P, B])
    sig = sb(sa, "sig", [P, B])
    wmod = sb(sa, "wmod", [P, 6 * D])
    wdq = sb(sa, "wdq", [P, AQ])
    wdkv = sb(sa, "wdkv", [P, AQ])
    wq3 = sb(sa, "wq3", [AQ, 3, D])
    wuk = sb(sa, "wuk", [AQ, D])
    wk2 = sb(sa, "wk2", [P, 2, D])
    wuv = sb(sa, "wuv", [AQ, D])
    wo_a = sb(sa, "wo_a", [P, D])
    bv = sb(sa, "bv", [P, D])
    ropec = sb(sa, "ropec", [P, T])
    ropes = sb(sa, "ropes", [P, T])
    selg = sb(sa, "selg", [P, NG, P])
    msel = sb(sa, "msel", [AH, NG, P])
    onesc = sb(sa, "onesc", [P, 1])
    lam = sb(sa, "lam", [P, 2])
    hT = sb(sa, "hT", [P, T])
    ctq = sb(sa, "ctq", [AQ, T])
    ctkv = sb(sa, "ctkv", [AQ, T])
    rot = sb(sa, "rot", [P, 3, T])
    qkT = sb(sa, "qkT", [P, 2, 2, T])
    hi = sb(sa, "hi", [P, T], F32R)
    q3 = sb(sa, "q3", [P, 2, NG, T], F32R)
    k3 = sb(sa, "k3", [P, 2, NG, T], F32R)
    q3m = sb(sa, "q3m", [P, NG, T], F32R)
    vtok = sb(sa, "vtok", [P, 2, TT, AH, 32])
    mx = sb(sa, "mx", [P, TT, AH])
    nmT = sb(sa, "nmT", [AH, T])
    pT = sb(sa, "pT", [P, 2, TT, T])
    oG = sb(sa, "oG", [P, T])
    rden = sb(sa, "rden", [P, TT, AG])
    otok = sb(sa, "otok", [P, TT, AH, AD])
    oT = sb(sa, "oT", [P, T])
    yT = sb(sa, "yT", [P, T])

    loads = [(x0[:, :, :], a["x"].rearrange("b (t p) d -> p (b t) d", p=P)),
             (cT[:, :], a["cT"]), (wmod[:, :], a["wmod"]), (wdq[:, :], a["wdq"]), (wdkv[:, :], a["wdkv"]),
             (wq3[:, :, :], a["wq3"].rearrange("w k n -> k w n")), (wuk[:, :], a["wuk"]),
             (wk2[:, :, :], a["wk2"].rearrange("w k n -> k w n")), (wuv[:, :], a["wuv"]),
             (wo_a[:, :], a["wo_a"]), (bv[:, :], a["bv"].rearrange("(o n) -> o n", o=1).broadcast_to([P, D])),
             (ropec[:, :], a["ropec"]), (ropes[:, :], a["ropes"]),
             (selg[:, :, :], a["selg"]), (msel[:, :, :], a["msel"]), (onesc[:, :], a["onesc"]),
             (lam[:, :], a["lam"])]
    NX = 3
    for n, (dst, src) in enumerate(loads):
        sp.dma(lambda e, d=dst, s=src: e.dma_start(d, s), s_x if n < NX else s_a)
    x_loaded, loaded = (s_x, 16 * NX), (s_a, 16 * (len(loads) - NX))

    eps_set = pool.do(lambda e: e.memset(epsc[:, :], EPS))
    m = pool.do(lambda e: e.memset(vtok[:, :, :, :, :], 0.0))
    mx_zero = pool.do(lambda e: e.memset(mx[:, :, :], 0.0))
    v_ones = pool.do(lambda e: e.memset(vtok[:, :, :, :, AD:AD + 1], 1.0), m)
    ring = Banks([bank(4), bank(5), bank(7)])

    m = act.do(lambda e: e.activation(sig[:, :], cT[:, :], ACT.Exp, scale=-1.0), x_loaded)
    m = dve.do(lambda e: e.tensor_scalar(sig[:, :], sig[:, :], 1.0, None, ALU.add), m, x_loaded)
    m = dve.do(lambda e: e.reciprocal(sig[:, :], sig[:, :]), m)
    m = dve.do(lambda e: e.tensor_tensor(sig[:, :], sig[:, :], cT[:, :], ALU.mult), m)
    i, bk, _ = ring.take()
    for j in range(6):
        mm = pe.do(lambda e, j=j, bk=bk: e.matmul(bk[:, j * B:(j + 1) * B], wmod[:, j * D:(j + 1) * D], sig[:, :],
                                                  start=True, stop=True), m, x_loaded, signal=j == 5)
    mod_v = mod[:, :, :].rearrange("p j b -> p (j b)")
    m = dve.do(lambda e, bk=bk: e.tensor_copy(mod_v, bk[:, 0:6 * B]), mm)
    ring.free[i] = m
    gate, sgn, mag = mod[:, 2::3, :], rot[:, 0, 0:2 * B], rot[:, 1, 0:2 * B]
    sgn, mag = (v.rearrange("p (j b) -> p j b", b=B) for v in (sgn, mag))
    m = dve.do(lambda e: e.tensor_scalar(mod[:, 1::3, :], mod[:, 1::3, :], 1.0, None, ALU.add), m)
    m = dve.do(lambda e: e.tensor_scalar(sgn, gate, 0.0, 2.0, ALU.is_ge, ALU.mult), m)
    m = dve.do(lambda e: e.scalar_tensor_tensor(out=mag, in0=gate, scalar=-1.0, in1=gate, op0=ALU.mult,
                                                op1=ALU.max), m)
    m = dve.do(lambda e: e.tensor_scalar(mag, mag, 0.25, None, ALU.max), m)
    m = dve.do(lambda e: e.scalar_tensor_tensor(out=gate, in0=sgn, scalar=-1.0, in1=mag, op0=ALU.add,
                                                op1=ALU.mult), m)
    mod_ready = m

    q_free = [None, None]
    state = {}

    def prepare(b):
        par = b % 2
        x_tile = lambda t: x0[:, b * TT + t, :]
        i, bk, free = ring.take()
        m = transpose_tiles(bk, x_tile, after=[x_loaded, free])
        ring.free[i] = act.do(lambda e, bk=bk: e.copy(xT[:, b, :], bk), m)
        yield
        m = normalise(x_tile, x_loaded)
        yield
        i, bk, free = ring.take()
        m = transpose_tiles(bk, lambda t: xn[:, t, :], after=[m, free])
        xn_free[0] = m
        h = act.do(lambda e, bk=bk: e.activation(hT[:, :], bk, ACT.Identity, bias=mod[:, 0, b:b + 1],
                                          scale=mod[:, 1, b:b + 1]), m, mod_ready, state.get("h_read"))
        ring.free[i] = h
        yield
        ct = []
        for w, dst, key in ((wdq, ctq, "b_dq"), (wdkv, ctkv, "b_dkv")):
            i, bk, free = ring.take()
            m = pe.do(lambda e, w=w, bk=bk: e.matmul(bk[0:AQ, :], w[:, :], hT[:, :], start=True, stop=True),
                      h, free, loaded)
            m = act.do(lambda e, bk=bk, dst=dst, key=key: e.activation(dst[:, :], bk[0:AQ, :], ACT.Identity,
                                                                       bias=vec(key, AQ)), m,
                       state.get("ct_read"))
            ring.free[i] = m
            ct.append(m)
            yield
        for n, (names, ws, srcs) in enumerate((
                (("bq_c", "bq_r", "bq_s"), (wq3[:, 0, :], wq3[:, 1, :], wq3[:, 2, :]), (ctq, ctq, ctq)),
                (("bk_c", "bk_r", "bk_s"), (wuk[:, :], wk2[:, 0, :], wk2[:, 1, :]), (ctkv, hT, hT)))):
            r = []
            for j in (1, 2, 0):
                i, bk, free = ring.take()
                m = pe.do(lambda e, bk=bk, w=ws[j], s=srcs[j]: e.matmul(bk, w, s[:, :], start=True, stop=True),
                          ct, free)
                if j:
                    tab = ropec if j == 1 else ropes
                    m = dve.do(lambda e, bk=bk, j=j, tab=tab, key=names[j]: e.scalar_tensor_tensor(
                        out=rot[:, j, :], in0=bk, scalar=vec(key), in1=tab[:, :], op0=ALU.add, op1=ALU.mult),
                        m, dve.last())
                else:
                    m = dve.do(lambda e, bk=bk, key=names[0]: e.scalar_tensor_tensor(
                        out=rot[:, 0, :], in0=bk, scalar=vec(key), in1=rot[:, 1, :], op0=ALU.add, op1=ALU.add),
                        m, r)
                ring.free[i] = m
                r.append(m)
                yield
            state["qk", par, n] = dve.do(lambda e, n=n: e.tensor_tensor(qkT[:, par, n, :], rot[:, 0, :],
                                                                        rot[:, 2, :], ALU.add), r, q_free[par])
        i, bk, free = ring.take()
        for t in range(TT):
            m = pe.do(lambda e, t=t, bk=bk: e.matmul(bk[:, t * P:(t + 1) * P], ctkv[:, t * P:(t + 1) * P],
                                                     wuv[:, :], start=True, stop=True), free, signal=t == TT - 1)
        state["ct_read"] = state["h_read"] = m
        bv_all = bv[:, :].rearrange("p (o h d) -> p o h d", o=1, h=AH).broadcast_to([P, TT, AH, AD])
        m = dve.do(lambda e, bk=bk: e.tensor_tensor(
            vtok[:, par, :, :, 0:AD], bk.rearrange("p (t h d) -> p t h d", t=TT, h=AH), bv_all, ALU.add),
            m, v_ones, state.get(("v_read", par)))
        ring.free[i] = state["v", par] = m
        yield
        for g in range(NG):
            state["q3", par, g] = pack(q3[:, par, g, :], par, 0, g, state.get(("q3_read", par)))
            yield
            state["packed", par, g] = pack(k3[:, par, g, :], par, 1, g, state.get(("k3_read", par)))
            yield

    def pack(dst, par, n, g, free_dst):
        i, bk, free = ring.take()
        m = pe.do(lambda e: e.matmul(bk, selg[:, g, :], qkT[:, par, n, :], start=True, stop=True), state["qk", par, n],
                  free)
        q_free[par] = m
        bias = onesc[:, 0:1] if n else 0.0
        h = act.do(lambda e: e.activation(hi[:, :], bk, ACT.Identity, bias=bias), m, state.get("hi_read"))
        m = dve.do(lambda e: e.scalar_tensor_tensor(out=dst, in0=hi[:, :].bitcast(F32), scalar=lam[:, n:n + 1],
                                                    in1=bk, op0=ALU.mult, op1=ALU.add), h, free_dst)
        state["hi_read"] = m
        ring.free[i] = m
        return m

    def maxima(b, h):
        par, g, r = b % 2, h // AG, 32 * (h % AG)
        for t in range(TT):
            i, bk, free = ring.take()
            m = pe.do(lambda e, t=t, bk=bk: e.matmul(bk, q3[r:r + 32, par, g, t * P:(t + 1) * P], k3[r:r + 32, par, g, :],
                                                     start=True, stop=True), state["packed", par, g], free)
            ring.free[i] = dve.do(lambda e, t=t, bk=bk: e.tensor_reduce(mx[:, t, h:h + 1], bk, AX_X, ALU.max),
                                  m, state.get("mx_read"), mx_zero)
            state["mx"] = ring.free[i]
            yield

    def spread_maxima():
        i, bk, free = ring.take()
        for t in range(TT):
            m = pe.do(lambda e, t=t: e.transpose(bk[0:AH, t * P:(t + 1) * P], mx[:, t, :], ident[:, :]),
                      state["mx"], free, signal=t == TT - 1)
        state["mx_read"] = m
        state["nm"] = ring.free[i] = act.do(lambda e: e.mul(nmT[:, :], bk[0:AH, :], -1.0), m, state.get("nm_read"))

    def pack_with_maxima(b, g):
        par = b % 2
        i, bk, free = ring.take()
        m = pe.do(lambda e: e.matmul(bk, msel[:, g, :], nmT[:, :], start=True, stop=True), state["nm"], free)
        state["nm_read"] = m
        m = dve.do(lambda e: e.tensor_tensor(q3m[:, g, :], q3[:, par, g, :].bitcast(F32), bk, ALU.add), m,
                   state["q3", par, g], state.get(("q3m_read", g)))
        ring.free[i] = state["packed_m", g] = state["q3_read", par] = m

    score_free = [None, None]
    pT_free = [None, None]
    exps = {}

    def exponentials(b, h):
        par, g, r = b % 2, h // AG, 32 * (h % AG)
        for half in range(2):
            for c in range(2 * half, 2 * half + 2):
                m = pe.do(lambda e, c=c: e.matmul(bank(c), k3[r:r + 32, par, g, c * P:(c + 1) * P],
                                                  q3m[r:r + 32, g, :], start=True, stop=True),
                          state["packed_m", g], score_free[half], signal=c % 2 == 1)
            m = act.do(lambda e, half=half: e.activation(pT[:, h % 2, 2 * half:2 * half + 2, :],
                                                         psum[:, 2 * half:2 * half + 2, :], ACT.Exp,
                                                         scale=1.0 / float(np.sqrt(np.float32(AH + AQ + AQ)))),
                       m, pT_free[h % 2])
            score_free[half] = m
        exps[h] = m
        state["q3m_read", g] = pe.last()
        if h == AH - 1:
            state["k3_read", par] = pe.last()

    out_free = [None]

    def weighted(b, h):
        par, g, hh = b % 2, h // AG, h % AG
        o = bank(6)
        for c in range(TT):
            yield
            m = pe.do(lambda e, c=c: e.matmul(o[32 * hh:32 * hh + 32, :], vtok[:, par, c, h, :], pT[:, h % 2, c, :],
                                              start=c == 0, stop=c == TT - 1, skip_group_check=True),
                      exps[h], state["v", par], out_free[0], signal=c == TT - 1)
        pT_free[h % 2] = m
        if h == AH - 1:
            state["v_read", par] = m
        if hh == AG - 1:
            state["sums", g] = out_free[0] = act.do(lambda e: e.copy(oG[:, :], o), m, state.get("oG_read"))

    def divide(b, g):
        i, bk, free = ring.take()
        m = transpose_tiles(bk, lambda t: oG[:, t * P:(t + 1) * P], after=[state["sums", g], free])
        state["oG_read"] = m
        o = bk.rearrange("p (t h c) -> p t h c", t=TT, h=AG)
        r = dve.do(lambda e: e.reciprocal(rden[:, :, :], o[:, :, :, AD]), m, state.get("rden_read"))
        den = rden[:, :, :].rearrange("p t (h o) -> p t h o", o=1).broadcast_to([P, TT, AG, AD])
        hs = slice(g * AG, g * AG + AG)
        m = dve.do(lambda e: e.tensor_tensor(otok[:, :, hs, :], o[:, :, :, 0:AD], den, ALU.mult), r,
                   state.get("otok_read"))
        ring.free[i] = state["otok"] = state["rden_read"] = m

    def finish_attention(b):
        i, bk, free = ring.take()
        m = transpose_tiles(bk, lambda t: otok[:, t, :, :].rearrange("p h d -> p (h d)"), after=[state["otok"], free])
        state["otok_read"] = m
        m = ring.free[i] = act.do(lambda e, bk=bk: e.copy(oT[:, :], bk), m)
        yield
        i, bk, free = ring.take()
        m = pe.do(lambda e, bk=bk: e.matmul(bk, wo_a[:, :], oT[:, :], start=True, stop=True), m, free)
        m = ring.free[i] = dve.do(lambda e, bk=bk: e.tensor_scalar(yT[:, :], bk, vec("b_o"), mod[:, 2, b:b + 1],
                                                                   ALU.add, ALU.mult), m)
        m = dve.do(lambda e: e.tensor_tensor(xT[:, b, :], xT[:, b, :], yT[:, :], ALU.add), m, act.last())
        yield
        i, bk, free = ring.take()
        m = transpose_tiles(bk, lambda t: xT[:, b, t * P:(t + 1) * P], after=[m, free])
        m = ring.free[i] = normalise(lambda t, bk=bk: bk[:, t * P:(t + 1) * P], m)
        yield
        i, bk, free = ring.take()
        m = transpose_tiles(bk, lambda t: xn[:, t, :], after=[m, free])
        xn_free[0] = m
        ring.free[i] = act.do(lambda e, bk=bk: e.activation(rT[:, b, :], bk, ACT.Identity, bias=mod[:, 3, b:b + 1],
                                                            scale=mod[:, 4, b:b + 1]), m)

    for _ in prepare(0):
        pass
    for h in range(AG):
        for _ in maxima(0, h):
            pass
    finishing = iter(())
    for b in range(B):
        following = prepare(b + 1) if b + 1 < B else iter(())
        spread_maxima()
        pack_with_maxima(b, 0)
        for h in range(AH + 1):
            if h < AH:
                exponentials(b, h)
            group_ends = h % AG == AG - 1 and h + 1 < AH
            if group_ends and b:
                pack_with_maxima(b, h // AG + 1)
            tiles = []
            if b == 0 and h + AG < AH:
                tiles += [maxima(0, h + AG)]
            if b + 1 < B and AH // 2 <= h < AH:
                for _ in following:
                    pass
                tiles += [maxima(b + 1, 2 * h - AH), maxima(b + 1, 2 * h - AH + 1)]
            tiles = (None for g in tiles for _ in g)
            for c, _ in enumerate(weighted(b, h - 1) if h else range(TT)):
                next(tiles, None)
                next(tiles, None)
                if h < AH // 2 and c < TT - 1:
                    next(following, None)
            for _ in tiles:
                pass
            if group_ends and b == 0:
                spread_maxima()
                pack_with_maxima(b, h // AG + 1)
            if h % AG == 1 and h > AG and h < AH:
                divide(b, h // AG - 1)
            if h > 1:
                next(finishing, None)
        divide(b, NG - 1)
        finishing = finish_attention(b)
    for _ in finishing:
        pass
    sa.close()

    ends = start_stage("B")
    identb = sb(ctx, "identb", [P, P], BF16)
    masks = sb(ctx, "masks", [P, 2, 512], BF16)
    tabs = sb(ctx, "tabs", [P, 4, T])
    GT = 4
    pairsel = sb(ctx, "pairsel", [P, GT, 2 * GT])
    WCH = INNER // 2
    w_raw = sb(ctx, "w_raw", [P, 2, WCH])
    wqk_hi = sb(ctx, "wqk_hi", [P, 2, 2, WCH], F32R)
    wqk_lo = sb(ctx, "wqk_lo", [P, 2, 2, WCH], F32R)
    wv_hi = sb(ctx, "wv_hi", [P, 2, WCH], F32R)
    wv_lo = sb(ctx, "wv_lo", [P, 2, WCH], F32R)
    wo = sb(ctx, "wo", [P, HP, D])
    w1_hi = sb(ctx, "w1_hi", [P, 2 * DI], F32R)
    w1_lo = sb(ctx, "w1_lo", [P, 2 * DI], F32R)
    w2 = sb(ctx, "w2", [P, NC, D])
    xs = sb(ctx, "xs", [P, T])
    xs_hi = sb(ctx, "xs_hi", [P, 2, WIN + T], F32R)
    xs_lo = sb(ctx, "xs_lo", [P, 2, WIN + T], F32R)
    NRAW, NSWAP = 4, 4
    raw = sb(ctx, "raw", [P, NRAW, T])
    swapped = sb(ctx, "swapped", [P, NSWAP, T])
    sq = sb(ctx, "sq", [P, 2, T])
    u = sb(ctx, "u", [P, 2 * GT, T])
    nsq = sb(ctx, "nsq", [2 * GT, T])
    rn = sb(ctx, "rn", [P, 2, TT, 2 * GT])
    mhalf = sb(ctx, "mhalf", [P, TT * 2 * GT])
    rn2 = sb(ctx, "rn2", [P, TT, 4 * GT])
    rnT = sb(ctx, "rnT", [4 * GT, 2, T], F32R)
    selr = sb(ctx, "selr", [4 * GT, GT, P], F32R)
    qz = sb(ctx, "qz", [P, HP, NWIN, 2, WIN])
    kT = sb(ctx, "kT", [P, HP, WIN + T])
    HU = H // 2
    MU = HU // 2
    v1 = sb(ctx, "v1", [P, 2, HU, DH + 1])
    v0 = sb(ctx, "v0", [P, 2, HU, DH + 1])
    smax = sb(ctx, "smax", [P, HU])
    sdiff = sb(ctx, "sdiff", [P, HU, 2 * WIN])
    px = sb(ctx, "px", [P, HU, P])
    pxT = sb(ctx, "pxT", [P, HU, P])
    rd = sb(ctx, "rd", [P, HU])
    on = sb(ctx, "on", [P, HU, DH])
    onT = sb(ctx, "onT", [P, MU, P])
    hn_hi = sb(ctx, "hn_hi", [P, T], F32R)
    hn_lo = sb(ctx, "hn_lo", [P, T], F32R)
    gel = sb(ctx, "gel", [P, T])
    hid = sb(ctx, "hid", [P, NC, T])
    hn = hid[:, 0, :]

    cb = [(u[:, 1:3, :], a["masks"]), (tabs[:, :, :], a["tabs"]),
          (pairsel[:, :, :], a["pairsel"]), (u[0:4 * GT, 0, :], a["selr"].rearrange("k g p -> k (g p)"))]
    s_cb = sem("s_cb")
    sp.wait(ends)
    constb = (s_cb, 16 * len(cb))

    landed = [0, 0]
    raw_free = [None, None]
    w_marks = {}

    def load_piece(src):
        half, n = state["half"], src.shape[1]
        state["half"] = 1 - half
        sp.dma(lambda e: e.dma_start(w_raw[:, half, 0:n], src), s_wraw[half], raw_free[half])
        landed[half] += 16
        return half, n, (s_wraw[half], landed[half])

    def split_piece(key, piece, hi_, lo_, free, eng=pool):
        half, n, ready = piece
        m = eng.do(lambda e: e.tensor_copy(hi_, w_raw[:, half, 0:n]), ready, free)
        m = eng.do(lambda e: e.tensor_tensor(lo_, w_raw[:, half, 0:n], hi_.bitcast(F32), ALU.subtract), m)
        w_marks[key] = raw_free[half] = m

    state["half"] = 0

    def weight_piece(i, kind, half):
        if kind == "v":
            dst = [w[:, half, :] for w in (wv_hi, wv_lo)]
            return (("v", half), a["wqkv"][i, :, 2 * INNER + half * WCH:2 * INNER + (half + 1) * WCH], *dst)
        if kind == "w1":
            c0, c1 = half * DI, (half + 1) * DI
            return (("w1", half), a["w1"][i, :, c0:c1], w1_hi[:, c0:c1], w1_lo[:, c0:c1])
        c0 = kind * INNER + half * WCH
        return ((kind, half), a["wqkv"][i, :, c0:c0 + WCH], wqk_hi[:, kind, half, :], wqk_lo[:, kind, half, :])

    def load_wo(i, half, *after):
        sp.dma(lambda e: e.dma_start(wo[:, half * HP // 2:(half + 1) * HP // 2, :],
                                     a["wo"][i, half * WCH:(half + 1) * WCH].rearrange("(m p) d -> p m d", p=P)),
               s_wo[half], after)

    def load_w2(i, *after):
        for c, (c0, n) in enumerate(DI_CHUNKS):
            sp.dma(lambda e, c=c, c0=c0, n=n: e.dma_start(w2[0:n, c, :], a["w2"][i, c0:c0 + n, :]), s_w2, after)

    first = ((0, 0), (1, 0), (0, 1), (1, 1), ("v", 0), ("v", 1), ("w1", 0), ("w1", 1))
    loaded_first = [load_piece(weight_piece(0, *key)[1]) for key in first[:2]]
    for dst, src in cb:
        sp.dma(lambda e, d=dst, s=src: e.dma_start(d, s), s_cb)

    def fill(eng, *views, value=0.0):
        for t_ in views:
            m = eng.do(lambda e, t_=t_: e.memset(t_.bitcast(F32) if t_.dtype == F32R else t_, value))
        return m

    qz_zero = fill(dve, qz[:, :, :, :, :])
    px_zero = fill(dve, px[:, :, :])
    s_v0, v0_in = [sem("s_v0_0"), sem("s_v0_1")], [0, 0]
    pads = fill(pool, xs[:, 0:1], xs_hi[:, :, 0:WIN + 1], xs_lo[:, :, 0:WIN + 1], kT[:, :, 0:WIN])
    selr_ready = pool.do(lambda e: e.tensor_copy(selr[:, :, :].rearrange("k g p -> k (g p)"), u[0:4 * GT, 0, :]), constb)
    pool.do(lambda e: e.tensor_copy(masks[:, :, :], u[:, 1:3, :]), constb)
    masks_ready = pool.do(lambda e: e.tensor_copy(identb[:, :], ident[:, :]), consts)
    fill(pool, mhalf[:, :], value=-0.5)
    v1_ones = fill(pool, v1[:, :, :, DH:DH + 1], value=1.0)

    def first_piece(n):
        key, src, hi_, lo_ = weight_piece(0, *first[n])
        split_piece(key, loaded_first[n], hi_, lo_, None, dve)
        if n + 2 < len(first):
            loaded_first.append(load_piece(weight_piece(0, *first[n + 2])[1]))

    first_piece(0)
    first_piece(1)
    load_wo(0, 0)
    load_wo(0, 1)
    load_w2(0)

    def do_mm3(o, lhs, rhs, *after, signal=True):
        pe.do(lambda e: e.matmul(o, lhs[0], rhs[0], start=True, stop=False), *after, signal=False)
        pe.do(lambda e: e.matmul(o, lhs[0], rhs[1], start=False, stop=False), signal=False)
        return pe.do(lambda e: e.matmul(o, lhs[1], rhs[0], start=False, stop=True), signal=signal)

    st = {}

    halves = ((slice(0, 64), 0), (slice(64, P), 1))

    def shift(b):
        for rows, late in halves:
            m = act.do(lambda e, rows=rows, late=late: e.copy(xs[rows, late:], rT[rows, b, 0:T - late]), st.get(("res", b)),
                       st.get("xs_read"), pads)
        return m

    def shift_parts(b):
        free = st.get(("xsp_read", b % 2))
        for rows, late in halves:
            hi_, lo_ = (w[rows, b % 2, WIN + late:] for w in (xs_hi, xs_lo))
            r = rT[rows, b, 0:T - late]
            h_ = act.do(lambda e, hi_=hi_, r=r: e.copy(hi_, r), st.get(("res", b)), free, pads)
            m = dve.do(lambda e, hi_=hi_, lo_=lo_, r=r: e.tensor_tensor(lo_, r, hi_.bitcast(F32), ALU.subtract), h_,
                       st.get(("res", b)), free)
        return m

    bank_free = [None] * 8
    s_swap = [sem(f"s_swap{k}") for k in range(NSWAP // 2)]
    swaps = [0] * (NSWAP // 2)
    u_free = [masks_ready] * (2 * GT)
    UT = 2 * MU

    LT = 2 * B * UT
    LB = 2 * B * TT

    def tile(n):
        i, n = divmod(n, LT)
        k, j = divmod(n, UT)
        return i, k // 2, k % 2, j // MU, (k % 2) * MU + j % MU

    NT = DEPTH * LT
    LAG = GT + 4

    def project():
        SUMS = 2
        NORM = 3
        marks = {}

        def heads(n):
            i, b, half, which, m_ = tile(n)
            x_ = (xs_hi[:, b % 2, WIN:], xs_lo[:, b % 2, WIN:])
            bk, slot, j, r_, s_ = n % 2, n % (2 * GT), n % 2, n % NRAW, n % NSWAP
            cols = slice((m_ % MU) * P, (m_ % MU + 1) * P)
            m = do_mm3(bank(bk), (wqk_hi[:, which, half, cols], wqk_lo[:, which, half, cols]), x_, marks["xs", b],
                       w_marks[which, half], bank_free[bk])
            st["wqk_read", which, half] = m
            c = marks["raw", n] = act.do(lambda e: e.mul(raw[:, r_, :], bank(bk), vec(("ks" if which else "qs", i))), m,
                                         st.get(("raw_read", r_)))
            bank_free[bk] = marks["sq", n] = act.do(lambda e: e.activation(sq[:, j, :], bank(bk), ACT.Square), m,
                                                    st.get(("sq_read", j)))
            a_ = dve.do(lambda e: e.tensor_tensor(u[:, slot, :], raw[:, r_, :], tabs[:, 2 * which, :], ALU.mult), c,
                        constb, u_free[slot])
            marks["cos", n] = st["raw_read", r_] = [a_]

        def swap(n):
            r_, s_ = n % NRAW, n % NSWAP
            for hp in range(2):
                for half in range(2):
                    f, t_ = 64 * hp + 32 * half, 64 * hp + 32 * (1 - half)
                    sp.dma(lambda e, f=f, t_=t_: e.dma_start(swapped[t_:t_ + 32, s_:s_ + 2, :],
                                                             raw[f:f + 32, r_:r_ + 2, :]),
                           s_swap[s_ // 2], marks["raw", n], marks["raw", n + 1], st.get(("swapped_read", s_)),
                           st.get(("swapped_read", s_ + 1)))
            swaps[s_ // 2] += 64
            for k in range(2):
                marks["swap", n + k] = (s_swap[s_ // 2], swaps[s_ // 2])
                st["raw_read", r_ + k] = [marks["swap", n + k]] + st["raw_read", r_ + k]

        def rotate(n):
            which = tile(n)[3]
            slot, s_ = n % (2 * GT), n % NSWAP
            m = pool.do(lambda e: e.tensor_tensor(swapped[:, s_, :], swapped[:, s_, :], tabs[:, 2 * which + 1, :],
                                                 ALU.mult), marks["swap", n])
            marks["u", n] = st["swapped_read", s_] = pool.do(lambda e: e.tensor_tensor(
                u[:, slot, :], u[:, slot, :], swapped[:, s_, :], ALU.add), m, marks["cos", n])

        def square_sums(n):
            bk, k = SUMS, n % GT
            m = pe.do(lambda e: e.matmul(bank(bk)[0:2 * GT, :], pairsel[:, k, :], sq[:, n % 2, :], start=k == 0,
                                         stop=k == GT - 1), marks["sq", n], constb, bank_free[bk])
            st["sq_read", n % 2] = m
            if k == GT - 1:
                bank_free[bk] = marks["rows", n // GT] = act.do(
                    lambda e: e.copy(nsq[:, :], bank(bk)[0:2 * GT, :]), m, st.get("nsq_read"))

        def norms(g):
            bk = NORM
            src = bank(bk)[:, 0:TT * 2 * GT]
            for t in range(TT):
                m = pe.do(lambda e, t=t: e.transpose(src[:, t * 2 * GT:(t + 1) * 2 * GT], nsq[:, t * P:(t + 1) * P],
                                                     ident[0:2 * GT, 0:2 * GT]), marks["rows", g], bank_free[bk],
                          signal=t == TT - 1)
            st["nsq_read"] = m
            r3 = rn[:, g % 2, :, :]
            r = r3.rearrange("p t h -> p (t h)")
            m = bank_free[bk] = dve.do(lambda e: e.tensor_scalar(r, src, 1e-24, None, ALU.max), m,
                                       st.get(("rn_read", g % 2)))
            marks["norm", g] = pool.do(lambda e: e.tensor_tensor(r, r, mhalf[:, :], ALU.pow), m)

        def norm_parts(g):
            r3, r_hi, r_lo = rn[:, g % 2, :, :], rn2[:, :, 0:2 * GT], rn2[:, :, 2 * GT:]
            m = dve.do(lambda e: e.tensor_copy(r_hi.bitcast(F32R), r3), marks["norm", g], st.get("rn2_read"))
            m = dve.do(lambda e: e.tensor_tensor(r_lo, r3, r_hi, ALU.subtract), m)
            st["rn_read", g % 2] = marks["parts", g] = m

        def norm_rows(g):
            bk = NORM
            for t in range(TT):
                m = pe.do(lambda e, t=t: e.transpose(bank(bk)[0:4 * GT, t * P:(t + 1) * P], rn2[:, t, :], ident[:, :]),
                          marks["parts", g], bank_free[bk], signal=t == TT - 1)
            st["rn2_read"] = m
            marks["rn", g] = bank_free[bk] = act.do(lambda e: e.copy(rnT[:, g % 2, :], bank(bk)[0:4 * GT, :]), m,
                                                    st.get(("rnT_read", g % 2)))

        def scale(n):
            _, _, half, which, m_ = tile(n)
            g, k, slot = n // GT, n % GT, n % (2 * GT)
            bk = NORM
            m = pe.do(lambda e: e.matmul(bank(bk), selr[:, k, :], rnT[:, g % 2, :], start=True, stop=True),
                      marks["rn", g], bank_free[bk], selr_ready)
            st["rnT_read", g % 2] = m
            if which == 0:
                for hp in range(2):
                    s_ = slice(64 * hp, 64 * hp + 64)
                    m2 = dve.do(lambda e, s_=s_, hp=hp: e.tensor_tensor(
                        qz[s_, m_, :, hp, :], u[s_, slot, :].rearrange("p (w q) -> p w q", q=WIN),
                        bank(bk)[s_, :].rearrange("p (w q) -> p w q", q=WIN), ALU.mult), m, marks["u", n], qz_zero,
                                st.get(("qk_read", half)))
            else:
                m2 = dve.do(lambda e: e.tensor_tensor(kT[:, m_, WIN:], u[:, slot, :], bank(bk), ALU.mult), m,
                            marks["u", n], st.get(("qk_read", half)))
            bank_free[bk] = u_free[slot] = st["scaled", which, m_] = m2

        marks["xs", 0] = shift_parts(0)
        for n in range(NT + LAG):
            if n >= LAG:
                scale(n - LAG)
            if n % GT == 3 and GT < n <= NT + 3:
                norm_parts(n // GT - 1)
            if (n + 1) % (2 * UT) == 0 and n + 1 < NT:
                following = tile(n + 1)[1]
                marks["xs", following] = shift_parts(following)
            if n < NT:
                heads(n)
            if 1 <= n <= NT:
                square_sums(n - 1)
            if n % 2 == 0 and 4 <= n < NT + 4:
                rotate(n - 4)
                rotate(n - 3)
            if n % 2 == 1 and n < NT:
                swap(n - 1)
            if n % GT == 1 and GT < n <= NT + 1:
                norms(n // GT - 1)
            if n % GT == 3 and GT < n <= NT + 3:
                norm_rows(n // GT - 1)
            yield n

    ring = [0]

    def take():
        ring[0] += 1
        return 5 + ring[0] % 3

    def attention(pieces):
        mk = {}

        def where(n):
            i, n = divmod(n, LB)
            k, t = divmod(n, TT)
            return i, k // 2, k % 2, t

        def scores(n):
            _, _, half, t = where(n)
            first = 1 if t == 0 else 0
            pe.do(lambda e: e.matmul(bank(4), identb[:, :], masks[:, first, :], start=True, stop=False,
                                     skip_group_check=True), bank_free[4], masks_ready, signal=False)
            for j in range(MU):
                m_ = half * MU + j
                for s_ in range(2):
                    for w_ in range(2):
                        win = 4 * t + 2 * w_ + s_
                        o = bank(4)[64 * w_:64 * w_ + 64, (j * 2 + s_) * 64:][:, 0:64]
                        last = j == MU - 1 and s_ == 1 and w_ == 1
                        m = pe.do(lambda e, o=o, m_=m_, win=win, last=last: e.matmul(
                            o, qz[:, m_, win, :, :].rearrange("p h q -> p (h q)"), kT[:, m_, win * WIN:(win + 2) * WIN],
                            start=False, stop=last, skip_group_check=True),
                                  st["scaled", 0, m_], st["scaled", 1, m_], signal=last)
            if t == TT - 1:
                st["qk_read", half] = m
            sv = bank(4).rearrange("p (k j) -> p k j", j=2 * WIN)
            m = dve.do(lambda e: e.tensor_reduce(smax[:, :], sv, AX_X, ALU.max), m)
            mb = smax[:, :].rearrange("p (k o) -> p k o", o=1).broadcast_to([P, HU, 2 * WIN])
            m = dve.do(lambda e: e.tensor_tensor(sdiff[:, :, :], sv, mb, ALU.subtract), m, st.get("sdiff_read"))
            bank_free[4] = m
            for w_ in range(2):
                r = slice(64 * w_, 64 * w_ + 64)
                m2 = act.do(lambda e, r=r: e.activation(px[r, :, r], sdiff[r, :, :], ACT.Exp, scale=8.0), m,
                            st.get("px_read"), px_zero)
            st["sdiff_read"] = mk["px", n] = m2

        def values(n):
            i, b, half, t = where(n)
            par = n % 2
            now, before = v1[:, par, :, :], v1[:, 1 - par, :, :]
            bk = take()
            x_ = [p_[:, b % 2, WIN + t * P:WIN + (t + 1) * P] for p_ in (xs_hi, xs_lo)]
            m = do_mm3(bank(bk), x_, [w_[:, half, :] for w_ in (wv_hi, wv_lo)], w_marks["v", half],
                       bank_free[bk])
            st["wv_read", half] = m
            bank_free[bk] = c = mk["v1", n] = act.do(lambda e: e.copy(
                now[:, :, 0:DH], bank(bk).rearrange("p (h d) -> p h d", d=DH)), m, v1_ones, mk.get(("products", n - 2)),
                                                     mk.get(("v0", n - 1)))
            st["xsp_read", b % 2] = m
            free = mk.get(("products", n - 2))
            if t == 0:
                z = pool.do(lambda e: e.memset(v0[0:WIN, par, :, :], 0.0), free)
            else:
                z = None
                sp.dma(lambda e: e.dma_start(v0[0:WIN, par, :, :], before[P - WIN:P, :, :]), s_v0[par], mk["v1", n - 1],
                       free)
                v0_in[par] += 16
            sp.dma(lambda e: e.dma_start(v0[WIN:P, par, :, :], now[0:P - WIN, :, :]), s_v0[par], c, free)
            v0_in[par] += 16
            mk["v0", n] = [z, (s_v0[par], v0_in[par])]

        def transposes(n):
            for q in range(2):
                bk = take()
                for k in range(4):
                    m = pe.do(lambda e, k=k, q=q, bk=bk: e.transpose(bank(bk)[:, k * P:(k + 1) * P], px[:, 4 * q + k, :],
                                                                     ident[:, :]), mk["px", n], bank_free[bk],
                              signal=k == 3)
                eng = act if q == 0 else dve
                for hp in range(2):
                    dst = pxT[:, 4 * q:4 * q + 4, hp * 64:hp * 64 + 64].rearrange("p k (w q) -> p k w q", w=2)
                    src = bank(bk).rearrange("p (k w h q) -> p k w h q", w=2, h=2, q=WIN)[:, :, :, hp, :]
                    f = (lambda e, dst=dst, src=src: e.copy(dst, src)) if eng is act else \
                        (lambda e, dst=dst, src=src: e.tensor_copy(dst, src))
                    m2 = eng.do(f, m, mk.get(("products", n - 1)))
                mk["pxT", n, q] = bank_free[bk] = m2
            st["px_read"] = m

        def apply(n, g):
            bk = take()
            hs = slice(4 * g, 4 * g + 4)
            for h in range(4):
                j, hp = divmod(4 * g + h, 2)
                for s_ in range(2):
                    lhs = pxT[:, 2 * j + s_, hp * 64:hp * 64 + 64]
                    rhs = (v1 if s_ else v0)[:, n % 2, 4 * g + h, :]
                    o = bank(bk)[64 * s_:64 * s_ + 64, h * (DH + 1):(h + 1) * (DH + 1)]
                    m = pe.do(lambda e, o=o, lhs=lhs, rhs=rhs: e.matmul(o, lhs, rhs, start=True, stop=True),
                              mk["pxT", n, g], mk["v1", n], mk["v0", n], bank_free[bk], signal=h == 3 and s_ == 1)
            ov = bank(bk)[:, 0:4 * (DH + 1)].rearrange("p (h d) -> p h d", d=DH + 1)
            r = dve.do(lambda e: e.reciprocal(rd[:, hs], ov[:, :, DH]), m)
            den = rd[:, hs].rearrange("p (h o) -> p h o", o=1).broadcast_to([P, 4, DH])
            bank_free[bk] = mk["on", n, g] = dve.do(lambda e: e.tensor_tensor(on[:, hs, :], ov[:, :, 0:DH], den,
                                                                              ALU.mult), r, st.get("on_read"))
            if g:
                mk["products", n] = m

        def output(n):
            bk = take()
            for k in range(MU):
                m = pe.do(lambda e, k=k: e.transpose(
                    bank(bk)[:, k * P:(k + 1) * P], on[:, 2 * k:2 * k + 2, :].rearrange("p h d -> p (h d)"), ident[:, :]),
                          mk["on", n, 0], mk["on", n, 1], bank_free[bk], signal=k == MU - 1)
            bank_free[bk] = mk["onT", n] = act.do(lambda e: e.copy(onT[:, :, :].rearrange("p k c -> p (k c)"), bank(bk)),
                                                  m, st.get("onT_read"))
            st["on_read"] = m

        def product(n):
            i, b, half, t = where(n)
            bk = take()
            y = bank(bk)[:, 0:P]
            for j in range(MU):
                m = pe.do(lambda e, j=j: e.matmul(y, wo[:, half * MU + j, :], onT[:, j, :], start=j == 0, stop=j == MU - 1),
                          mk["onT", n], bank_free[bk], (s_wo[half], 16 * (i + 1)), signal=j == MU - 1)
            st["onT_read"] = st["wo_read", half] = m
            y_ = y.rearrange("p (s w q) -> p w s q", w=2, s=2)
            r = rT[:, b, t * P:(t + 1) * P].rearrange("p (w s q) -> p w s q", w=2, s=2)
            bank_free[bk] = st["res", b] = dve.do(lambda e: e.tensor_tensor(r, y_, r, ALU.add), m, dve.last())

        values(0)
        scores(0)
        N = DEPTH * LB
        for n in range(N):
            transposes(n)
            if n:
                output(n - 1)
            yield
            if n + 1 < N:
                scores(n + 1)
            pieces(n - 0.5)
            apply(n, 0)
            yield
            if n + 1 < N:
                values(n + 1)
            if n:
                product(n - 1)
            apply(n, 1)
            pieces(n)
        output(N - 1)
        product(N - 1)

    ff = {}

    def feed_forward(i, b):
        def shifted():
            ff["xs"] = shift(b)

        def token_major():
            m = ff["xs"]
            bk = take()
            m = transpose_tiles(bank(bk), lambda t: xs[:, t * P:(t + 1) * P], after=[m, bank_free[bk]])
            st["xs_read"] = m
            bank_free[bk] = ff["x"] = act.do(lambda e: e.copy(xn[:, :, :].rearrange("p t d -> p (t d)"), bank(bk)), m,
                                             xn_free[0])

        def statistics():
            for t in range(TT):
                m = dve.do(lambda e, t=t: e.bn_stats(stats[:, t, :], xn[:, t, :]), ff["x"], dve.last())
            for t in range(TT):
                m2 = dve.do(lambda e, t=t: e.bn_aggr(mv[:, t, :], stats[:, t, :]), m)
            m = pool.do(lambda e: e.tensor_scalar(rstd[:, :], mv[:, :, 1], EPS, None, ALU.add), m2)
            ff["rstd"] = pool.do(lambda e: e.tensor_tensor(rstd[:, :], rstd[:, :], mhalf[:, 0:TT], ALU.pow), m)

        def scaled():
            for t in range(TT):
                m = dve.do(lambda e, t=t: e.tensor_scalar(xn[:, t, :], xn[:, t, :], mv[:, t, 0:1], rstd[:, t:t + 1],
                                                          ALU.subtract, ALU.mult), ff["rstd"])
            ff["xn"] = m

        def feature_major():
            bk = take()
            m = transpose_tiles(bank(bk), lambda t: xn[:, t, :], after=[ff["xn"], bank_free[bk]])
            xn_free[0] = m
            m = act.do(lambda e: e.activation(hn, bank(bk), ACT.Identity, bias=vec(("b", i)), scale=vec(("g", i))),
                       m, st.get("hid_read"))
            bank_free[bk] = m
            h_ = act.do(lambda e: e.copy(hn_hi[:, :], hn), m, st.get("hns_read"))
            ff["h"] = dve.do(lambda e: e.tensor_tensor(hn_lo[:, :], hn, hn_hi[:, :].bitcast(F32), ALU.subtract), h_,
                             st.get("hns_read"))

        def up(c):
            c0, n = DI_CHUNKS[c]
            x_ = (hn_hi[:, :], hn_lo[:, :])
            kg, ka = take(), take()
            pa, pg = bank(ka)[0:n, :], bank(kg)[0:n, :]
            mg = do_mm3(pg, (w1_hi[:, DI + c0:DI + c0 + n], w1_lo[:, DI + c0:DI + c0 + n]), x_, ff["h"],
                        bank_free[kg], w_marks["w1", 0], w_marks["w1", 1])
            ma = do_mm3(pa, (w1_hi[:, c0:c0 + n], w1_lo[:, c0:c0 + n]), x_, bank_free[ka])
            g_ = act.do(lambda e: e.activation(gel[0:n, :], pg, ACT.Gelu, bias=vec(("b1g", i, c), n)), mg,
                        st.get("gel_read"))
            bank_free[kg] = g_
            bank_free[ka] = st["gel_read"] = ff["hid"] = dve.do(lambda e: e.scalar_tensor_tensor(
                out=hid[0:n, c, :], in0=pa, scalar=vec(("b1a", i, c), n), in1=gel[0:n, :], op0=ALU.add,
                op1=ALU.mult), ma, g_, ff["h"], st.get("hid_read"))
            st["hns_read"] = st["w1_read"] = ma

        def down():
            bk = take()
            for c, (c0, n) in enumerate(DI_CHUNKS):
                m = pe.do(lambda e, c=c, n=n: e.matmul(bank(bk), w2[0:n, c, :], hid[0:n, c, :], start=c == 0,
                                                       stop=c == NC - 1), ff["hid"], bank_free[bk],
                          (s_w2, 16 * NC * (i + 1)), signal=c == NC - 1)
            st["hid_read"] = st["w2_read"] = m
            bank_free[bk] = st["res", b] = dve.do(lambda e: e.scalar_tensor_tensor(
                out=rT[:, b, :], in0=bank(bk), scalar=vec(("b2", i)), in1=rT[:, b, :], op0=ALU.add, op1=ALU.add), m)

        return {0: shifted, 1: token_major, 2: statistics, 2.5: scaled, 3: feature_major,
                **{4 + c: (lambda c=c: up(c)) for c in range(NC)}, 4 + NC: down}

    def write_out(b):
        m = dve.do(lambda e: e.scalar_tensor_tensor(out=xT[:, b, :], in0=rT[:, b, :], scalar=mod[:, 5, b:b + 1],
                                                    in1=xT[:, b, :], op0=ALU.mult, op1=ALU.add), st["res", b])
        bk = take()
        m = transpose_tiles(bank(bk), lambda t: xT[:, b, t * P:(t + 1) * P], after=[m, bank_free[bk]])
        bank_free[bk] = m = act.do(lambda e: e.copy(xn[:, :, :].rearrange("p t d -> p (t d)"), bank(bk)), m, xn_free[0])
        sp.dma(lambda e: e.dma_start(out[b].rearrange("(t p) d -> p t d", p=P), xn[:, :, :]), s_out, m)
        xn_free[0] = (s_out, 16 * (b + 1))

    BATCH = 2 * TT
    blocks = {}
    staged = {}

    def at(n, fn):
        blocks.setdefault(n, []).append(fn)

    def stage_weights(n, i, kind, half, key):
        k_, src, hi_, lo_ = weight_piece(i, kind, half)

        def load():
            staged[k_] = load_piece(src)
        at(n, load)
        at(n + 1, lambda: split_piece(k_, staged[k_], hi_, lo_, st.get(key)))

    for i in range(DEPTH):
        for b in range(B):
            n = i * LB + (b + 1) * BATCH
            for k, piece in feed_forward(i, b).items():
                at(n + k, piece)
            if i == DEPTH - 1:
                at(n + 5 + NC, lambda b=b: write_out(b))
        if i + 1 == DEPTH:
            break
        n = (i + 1) * LB
        for half in range(2):
            stage_weights(n - 2 - (1 - half) * (TT - 1), i + 1, "v", half, ("wv_read", half))
            at(n + 1 - (1 - half) * TT, lambda i=i, half=half: load_wo(i + 1, half, st["wo_read", half]))
            for which in range(2):
                stage_weights(n - UT - (1 - half) * UT // 2 + which, i + 1, which, half, ("wqk_read", which, half))
            stage_weights(n + 1 + 3 + NC + half, i + 1, "w1", half, "w1_read")
        at(n + 2 + 3 + NC, lambda i=i: load_w2(i + 1, st["w2_read"]))

    def pieces(n):
        for fn in blocks.pop(n, []):
            fn()

    steps = project()
    for n in range(2 * UT + 1):
        next(steps)
        if n % 2 == 0 and 2 + n // 2 < len(first):
            first_piece(2 + n // 2)
    for _ in attention(pieces):
        next(steps, None)
    for n in sorted(blocks):
        pieces(n)
    sp.wait((s_out, 16 * B))

    block = ctx.enter_context(nc.Block())

    def run(steps):
        def body(e):
            for step in steps:
                step(e)
        return body

    block.tensor(run(pe.steps))
    block.vector(run(dve.steps))
    block.scalar(run(act.steps))
    block.gpsimd(run(pool.steps))
    block.sync(run(sp.steps))
    ctx.close()


def constants():
    f = np.float32
    c = {"ident": np.eye(P, dtype=f)}
    pos = np.arange(T, dtype=f)[:, None]
    ids = np.arange(D // 2, dtype=f)
    theta = (f(10000.0) ** (f(-2.0) * ids) / f(D // 2)).astype(f)
    r = (pos * theta[None, :]).astype(f)
    c["ropec"] = np.ascontiguousarray(np.repeat(np.cos(r), 2, axis=1).T)
    sgn = np.where(np.arange(D) % 2 == 0, -1, 1).astype(f)
    c["ropes"] = np.ascontiguousarray(np.repeat(np.sin(r), 2, axis=1).T * sgn[:, None])
    selg, msel, onesc = np.zeros((P, NG, P), f), np.zeros((AH, NG, P), f), np.zeros((P, 1), f)
    lam = np.zeros((P, 2), f)
    for g in range(NG):
        for h in range(AG):
            for k in range(3):
                for d in range(AD):
                    selg[(AG * g + h) * AD + d, g, 32 * h + AD * k + d] = 1
            msel[AG * g + h, g, 32 * h + 3 * AD] = 1
    for h in range(AG):
        onesc[32 * h + 3 * AD, 0] = lam[32 * h + 3 * AD, 1] = 1
        lam[32 * h + 2 * AD:32 * h + 3 * AD, 0] = -1
        lam[32 * h + AD:32 * h + 2 * AD, 1] = -1
    c.update(selg=selg, msel=msel, onesc=onesc, lam=lam)
    half = np.arange(0, DH, 2, dtype=f)
    inv_freq = (f(1.0) / f(10000.0) ** (half / f(DH))).astype(f)
    t = np.arange(T, dtype=f)
    fr = (t[:, None] * inv_freq[None, :]).astype(f)
    fr = np.concatenate([fr, fr], -1)
    base = ((half + f(0.4 * DH)) / f(1.4 * DH)).astype(f)
    power = ((t - T // 2) / f(WIN // 2)).astype(f)
    sc = (base[None, :] ** power[:, None]).astype(f)
    sc = np.concatenate([sc, sc], -1)
    inv = (f(1.0) / sc).astype(f)
    s2 = np.where(np.arange(DH) < DH // 2, -1, 1).astype(f)
    two = lambda z: np.tile(z.astype(f).T, (2, 1))
    c["tabs"] = np.ascontiguousarray(np.stack([two(np.cos(fr) * sc), two(np.sin(fr) * sc * s2),
                                               two(np.cos(fr) * inv), two(np.sin(fr) * inv * s2)], axis=1))
    pairsel = np.zeros((P, 4, 8), f)
    for k in range(4):
        pairsel[0:64, k, 2 * k] = 1
        pairsel[64:, k, 2 * k + 1] = 1
    c["pairsel"] = pairsel
    selr = np.zeros((16, 4, P), f)
    for k in range(4):
        for hp in range(2):
            for part in range(2):
                selr[8 * part + 2 * k + hp, k, 64 * hp:64 * hp + 64] = 1
    c["selr"] = selr
    q, j = np.arange(WIN)[:, None], np.arange(2 * WIN)[None, :]
    ok = (j >= q) & (j <= q + WIN)
    masks = np.zeros((P, 2, 4, 2, 2 * WIN), f)
    masks[:] = np.where(np.tile(ok, (4, 1)), 0.0, NEG)[:, None, None, None, :]
    masks[0:64, 1, :, 0, 0:WIN] = NEG
    c["masks"] = masks.reshape(P, 2, 512)
    return c


def kernel(**inputs):
    import concourse.bacc as bacc
    from concourse.bass_utils import run_bass_kernel_spmd

    x = {k.replace("L0_", ""): np.ascontiguousarray(v) for k, v in inputs.items()}
    pair = np.arange(D).reshape(-1, 2)[:, ::-1].reshape(-1)
    half = np.arange(DH).reshape(2, -1)[::-1].reshape(-1)
    arrays = constants()
    vecs = np.zeros((P, NVEC), np.float32)

    def put(key, v):
        vecs[0:len(v), VEC[key]] = v

    put("bq_c", x["attn_Wu_q_b"])
    put("bq_r", x["attn_Wq_r_b"])
    put("bq_s", x["attn_Wq_r_b"][pair])
    put("bk_c", x["attn_Wu_k_b"])
    put("bk_r", x["attn_Wk_r_b"])
    put("bk_s", x["attn_Wk_r_b"][pair])
    put("b_o", x["attn_Wo_b"])
    put("b_dq", x["attn_Wd_q_b"])
    put("b_dkv", x["attn_Wd_kv_b"])
    for i in range(DEPTH):
        for key, v in (("qs", x["ffn_q_scale"][i]), ("ks", x["ffn_k_scale"][i])):
            put((key, i), np.concatenate([v, v]))
        put(("g", i), x["ffn_ln_g"][i])
        put(("b", i), x["ffn_ln_b"][i])
        put(("b2", i), x["ffn_b2"][i])
        for c, (c0, n) in enumerate(DI_CHUNKS):
            put(("b1a", i, c), x["ffn_b1"][i, c0:c0 + n])
            put(("b1g", i, c), x["ffn_b1"][i, DI + c0:DI + c0 + n])
    arrays.update(
        vecs=vecs, x=x["attn_x"], cT=np.ascontiguousarray(x["c"].T), wmod=x["wmod"], wdq=x["attn_Wd_q_w"],
        wdkv=x["attn_Wd_kv_w"],
        wq3=np.stack([x["attn_Wu_q_w"], x["attn_Wq_r_w"], x["attn_Wq_r_w"][:, pair]]),
        wuk=x["attn_Wu_k_w"], wk2=np.stack([x["attn_Wk_r_w"], x["attn_Wk_r_w"][:, pair]]),
        wuv=x["attn_Wu_v_w"], wo_a=x["attn_Wo_w"], bv=x["attn_Wu_v_b"],
        wqkv=x["ffn_Wqkv"], wo=x["ffn_Wo"], w1=x["ffn_W1"],
        w2=x["ffn_W2"])
    nc = bacc.Bacc("TRN2", target_bir_lowering=False, num_devices=1)
    aps = {n: nc.dram_tensor(f"in_{n}", v.shape, mybir.dt.from_np(v.dtype), kind="ExternalInput").ap()
           for n, v in arrays.items()}
    out = nc.dram_tensor("out_x", (B, T, D), F32, kind="ExternalOutput").ap()
    build(nc, aps, out)
    r = run_bass_kernel_spmd(nc, [{f"in_{n}": v for n, v in arrays.items()}], core_ids=[0])
    return r.results[0]["out_x"]
```
